# Optimizing a Trainium2 kernel written in Bass

```python
import numpy as np
import jax
import jax.numpy as jnp

def _softmax(x, axis=-1):
    return jax.nn.softmax(x, axis=axis)

def _gelu(x):
    return jax.nn.gelu(x, approximate=True)

def _silu(x):
    return jax.nn.silu(x)

def _sigmoid(x):
    return jax.nn.sigmoid(x)

def _layernorm(x, axis=-1, eps=1e-05):
    m = jnp.mean(x, axis=axis, keepdims=True)
    v = jnp.var(x, axis=axis, keepdims=True)
    return (x - m) / jnp.sqrt(v + eps)

def _scatter_add(tgt, idx, src, axis=0):
    return tgt.at[idx].add(src)

def _segment_sum(src, seg, n):
    return jax.ops.segment_sum(src, seg, n)
kernel_name = 'mk_flamingo_gated_d1_seqx_r8_36428b'

def setup_inputs(seed: int=0):
    np.random.seed(seed)
    _w = jnp.asarray

    def _rec_inputs():
        import jax
        import jax.numpy as jnp
        _rk = jax.random.key(seed)
        x = 7.22e-05 + 1 * jax.random.normal(jax.random.fold_in(_rk, 1), (16, 64, 512), jnp.float32)
        _lenS = 64 - jax.random.randint(jax.random.fold_in(_rk, 7), (16,), 0, max(1, 64 // 4) + 1, jnp.int32)
        _lenS2 = 64 - jax.random.randint(jax.random.fold_in(_rk, 8), (16,), 0, max(1, 64 // 4) + 1, jnp.int32)
        _ctx_4096P = jax.random.normal(jax.random.fold_in(_rk, 11), (16, 16, 512), jnp.float32)
        _ctx_4096c = jax.random.dirichlet(jax.random.fold_in(_rk, 511), 0.3 * jnp.ones((16,), jnp.float32), (16, 64))
        _ctx_4096t = jnp.einsum('bsk,bkd->bsd', _ctx_4096c, _ctx_4096P)
        _ctx_4096t = _ctx_4096t * jax.lax.rsqrt(jnp.mean(jnp.square(_ctx_4096t)) + 1e-12) * 0.953939
        ctx_4096 = 4.13588e-05 + 0.999923 * (_ctx_4096t + 0.3 * jax.random.normal(jax.random.fold_in(_rk, 611), (16, 64, 512), jnp.float32))
        _g = jax.random.normal(jax.random.fold_in(_rk, 9001), (2, 1), jnp.float32)
        _g = jnp.sign(_g) * jnp.maximum(jnp.abs(_g), 1.0) + (_g == 0) * 1.0
        g_xattn = _g[0]
        g_ffn = _g[1]
        return (x, ctx_4096, g_xattn, g_ffn)
    x, ctx_4096, g_xattn, g_ffn = _rec_inputs()

    def _L0_xattn_setup():
        import jax, jax.numpy as jnp
        import numpy as np
        EPS = 1e-05

        def instance_norm(x):
            mu = jnp.mean(x, axis=-1, keepdims=True)
            var = jnp.mean((x - mu) ** 2, axis=-1, keepdims=True)
            return (x - mu) * jax.lax.rsqrt(var + EPS)
        key = jax.random.key(seed)
        ks = jax.random.split(key, 10)
        bs, qk_dim, v_dim, N, M = (4, 64, 64, 512, 512)
        sc_qk = 1.0 / np.sqrt(qk_dim)
        sc_v = 1.0 / np.sqrt(v_dim)
        return {'q': jax.random.normal(ks[0], (bs, qk_dim, N), jnp.float32), 'k': jax.random.normal(ks[1], (bs, qk_dim, M), jnp.float32), 'c': jax.random.normal(ks[2], (bs, v_dim, N), jnp.float32), 's': jax.random.normal(ks[3], (bs, v_dim, M), jnp.float32), 'Wq': jax.random.normal(ks[4], (qk_dim, qk_dim), jnp.float32) * sc_qk, 'bq': jax.random.normal(ks[5], (qk_dim,), jnp.float32) * 0.01, 'Wk': jax.random.normal(ks[6], (qk_dim, qk_dim), jnp.float32) * sc_qk, 'bk': jax.random.normal(ks[7], (qk_dim,), jnp.float32) * 0.01, 'Ws': jax.random.normal(ks[8], (v_dim, v_dim), jnp.float32) * sc_v, 'bs_': jax.random.normal(ks[9], (v_dim,), jnp.float32) * 0.01}
    _L0_xattn_all = _L0_xattn_setup()
    _L0_xattn_in = {k: v for k, v in _L0_xattn_all.items() if k in ('Wq', 'bq', 'Wk', 'bk', 'Ws', 'bs_')}
    del _L0_xattn_all

    def _L0_ffn_setup():
        import jax, jax.numpy as jnp
        import numpy as np
        IN_FEATURES = 512
        OUT_FEATURES = 512
        GROUPSIZE = 128
        N_GROUPS = IN_FEATURES // GROUPSIZE
        key = jax.random.key(seed)
        k1, k2, k3, k4 = jax.random.split(key, 4)
        x = jax.random.normal(k1, (4, 256, IN_FEATURES), dtype=jnp.float32)
        weight_q = jax.random.randint(k2, (OUT_FEATURES, IN_FEATURES), 0, 16, dtype=jnp.int32)
        scales = jax.random.uniform(k3, (N_GROUPS, OUT_FEATURES), dtype=jnp.float32) * 0.02 + 0.001
        zeros = jax.random.normal(k4, (N_GROUPS, OUT_FEATURES), dtype=jnp.float32) * 0.1
        scales_and_zeros = jnp.stack([scales, zeros], axis=-1)
        return {'input': x, 'weight_q': weight_q, 'scales_and_zeros': scales_and_zeros}
    _L0_ffn_all = _L0_ffn_setup()
    _L0_ffn_in = {k: v for k, v in _L0_ffn_all.items() if k in ('weight_q', 'scales_and_zeros')}
    del _L0_ffn_all
    return {'x': x, 'ctx_4096': ctx_4096, 'g_xattn': g_xattn, 'g_ffn': g_ffn, 'L0_xattn_Wq': _L0_xattn_in['Wq'], 'L0_xattn_bq': _L0_xattn_in['bq'], 'L0_xattn_Wk': _L0_xattn_in['Wk'], 'L0_xattn_bk': _L0_xattn_in['bk'], 'L0_xattn_Ws': _L0_xattn_in['Ws'], 'L0_xattn_bs_': _L0_xattn_in['bs_'], 'L0_ffn_weight_q': _L0_ffn_in['weight_q'], 'L0_ffn_scales_and_zeros': _L0_ffn_in['scales_and_zeros']}

def reference(x, ctx_4096, g_xattn, g_ffn, L0_xattn_Wq, L0_xattn_bq, L0_xattn_Wk, L0_xattn_bk, L0_xattn_Ws, L0_xattn_bs_, L0_ffn_weight_q, L0_ffn_scales_and_zeros):
    import jax
    import jax.numpy as jnp

    def _L0_xattn_ref(q, k, c, s, Wq, bq, Wk, bk, Ws, bs_):
        import jax, jax.numpy as jnp
        import numpy as np
        EPS = 1e-05

        def instance_norm(x):
            mu = jnp.mean(x, axis=-1, keepdims=True)
            var = jnp.mean((x - mu) ** 2, axis=-1, keepdims=True)
            return (x - mu) * jax.lax.rsqrt(var + EPS)
        qp = jnp.einsum('oc,bcn->bon', Wq, instance_norm(q)) + bq[None, :, None]
        kp = jnp.einsum('oc,bcm->bom', Wk, instance_norm(k)) + bk[None, :, None]
        sp = jnp.einsum('oc,bcm->bom', Ws, s) + bs_[None, :, None]
        attn = jax.nn.softmax(jnp.einsum('bcn,bcm->bnm', qp, kp), axis=-1)
        mean = jnp.einsum('bnm,bvm->bvn', attn, sp)
        mean_sq = jnp.einsum('bnm,bvm->bvn', attn, sp * sp)
        std = jnp.sqrt(jax.nn.relu(mean_sq - mean * mean))
        cs = instance_norm(c) * std + mean
        return cs

    def _L0_ffn_ref(input, weight_q, scales_and_zeros):
        import jax, jax.numpy as jnp
        import numpy as np
        IN_FEATURES = 512
        OUT_FEATURES = 512
        GROUPSIZE = 128
        N_GROUPS = IN_FEATURES // GROUPSIZE
        x = input.reshape(-1, IN_FEATURES)
        scales = scales_and_zeros[..., 0]
        zeros = scales_and_zeros[..., 1]
        q = weight_q.reshape(OUT_FEATURES, N_GROUPS, GROUPSIZE).astype(jnp.float32)
        w = q - 8.0
        w = w * scales.T[:, :, None] + zeros.T[:, :, None]
        w = w.reshape(OUT_FEATURES, IN_FEATURES)
        c = x @ w.T
        return c.reshape(input.shape[:-1] + (OUT_FEATURES,))
    x = x + jnp.tanh(g_xattn[0]) * _L0_xattn_ref(_layernorm(x, axis=-1), ctx_4096, ctx_4096, ctx_4096, L0_xattn_Wq, L0_xattn_bq, L0_xattn_Wk, L0_xattn_bk, L0_xattn_Ws, L0_xattn_bs_)
    x = x + jnp.tanh(g_ffn[0]) * _L0_ffn_ref(_layernorm(x, axis=-1), L0_ffn_weight_q, L0_ffn_scales_and_zeros)
    return x

_drawn_inputs = setup_inputs


def setup_inputs(seed=0):
    import zlib

    import numpy as np

    out = dict(_drawn_inputs(seed))
    spreads = {}
    factors = {'L0_xattn_bq': 3.122, 'L0_xattn_bk': 8.0, 'L0_xattn_bs_': 8.0}
    for name, (base, spread) in spreads.items():
        noise = np.random.default_rng([zlib.crc32(name.encode()), seed]).standard_normal(out[name].shape)
        drawn = base * np.exp(spread * noise) if base else spread * noise
        out[name] = jnp.asarray(drawn.astype(out[name].dtype))
    for name, factor in factors.items():
        out[name] = (out[name] * factor).astype(out[name].dtype)
    return out
```

```python
from contextlib import ExitStack

import concourse.bass as bass
from concourse import mybir

F32 = mybir.dt.float32
F32R = mybir.dt.float32r
I32 = mybir.dt.int32
ALU = mybir.AluOpType
ACT = mybir.ActivationFunctionType
AX_X = mybir.AxisListType.X

EPS = 1e-5
QUANT_ZERO = 8.0
P = 128


def gated_attention_ffn(nc, x, context, g_xattn, g_ffn, wq_t, bq, wk_t, bk, ws_t, bs,
                        weight_q_t, scales_zeros, out):
    BATCHES, C, N = x.shape
    TILES = BATCHES // 2
    JC = N // P
    CHUNKS = 2 * JC
    GROUPS = weight_q_t.shape[0] // P
    AHEAD_S, AHEAD_E = 3, 2
    SBANKS = 4
    LAST = CHUNKS * TILES
    DMA = 16
    STACK = 6 * DMA
    assert 2 * C == P and N == 512 and CHUNKS % SBANKS == 0

    x_tiles = x.rearrange("(t b) c n -> t (b c) n", b=2)
    context_tiles = context.rearrange("(t b) c n -> t (b c) n", b=2)
    out_tiles = out.rearrange("(t b) c n -> t (b c) n", b=2)

    with ExitStack() as ctx:
        def sb(name, shape, dt=F32):
            return ctx.enter_context(nc.sbuf_tensor(name, shape, dt))

        def bank(name):
            return ctx.enter_context(nc.psum_tensor(name, [P, 512], F32))

        def sem(name):
            return ctx.enter_context(nc.semaphore(name))

        X = sb("X", [P, TILES, N])
        CTX = sb("CTX", [P, TILES, N])
        XM = sb("XM", [P, TILES, N])
        VAR = sb("VAR", [P, TILES, N])
        w_qk = sb("w_qk", [P, 2, P])
        w_qk_hi = sb("w_qk_hi", [P, 2, P], F32R)
        w_qk_lo = sb("w_qk_lo", [P, 2, P], F32R)
        w_s = sb("w_s", [P, P])
        b_qk = sb("b_qk", [P, 2])
        b_s = sb("b_s", [P, C])
        xn = sb("xn", [P, N])
        x_hi = sb("x_hi", [P, N], F32R)
        x_lo = sb("x_lo", [P, N], F32R)
        c_hi = sb("c_hi", [P, N], F32R)
        c_lo = sb("c_lo", [P, N], F32R)
        ctx_now = sb("ctx_now", [P, N])
        stats = sb("stats", [P, 2, 6])
        mean_var = sb("mean_var", [P, 2, 2])
        var_eps = sb("var_eps", [P, 2])
        rstd = sb("rstd", [P, 2])
        q_hi = sb("q_hi", [P, N], F32R)
        q_lo = sb("q_lo", [P, N], F32R)
        k_hi = sb("k_hi", [P, N], F32R)
        k_lo = sb("k_lo", [P, N], F32R)
        q_stack = [sb(f"q_stack{b}", [P, N], F32R) for b in range(2)]
        k_same = [sb(f"k_same{b}", [P, N], F32R) for b in range(2)]
        k_cross = [sb(f"k_cross{b}", [P, N], F32R) for b in range(2)]
        probs = [sb(f"probs{i}", [P, N]) for i in range(SBANKS)]
        neg_max = sb("neg_max", [P, CHUNKS])
        den = sb("den", [P, CHUNKS])
        rden = sb("rden", [P, CHUNKS])
        probs_t = [sb(f"probs_t{b}", [P, JC, N]) for b in range(2)]
        values = sb("values", [P, JC, 2, 2, C])
        mean_sq = sb("mean_sq", [P, N])
        ident = sb("ident", [P, P])
        power = sb("power", [P, 2])
        gates = sb("gates", [P, 2])
        tanh_g = sb("tanh_g", [P, 2])
        w_int = sb("w_int", [P, GROUPS, N], I32)
        sz = sb("sz", [P, GROUPS, 2, N])
        w_deq = [sb(f"w_deq{i}", [P, N]) for i in range(2)]
        w_hi = sb("w_hi", [P, GROUPS, N], F32R)
        w_lo = sb("w_lo", [P, GROUPS, N], F32R)
        scaled = [sb(f"scaled{i}", [P, N]) for i in range(2)]
        stats2 = [sb(f"stats2{i}", [P, 6]) for i in range(2)]
        mean_var2 = [sb(f"mean_var2{i}", [P, 2]) for i in range(2)]
        var_eps2 = [sb(f"var_eps2{i}", [P, 1]) for i in range(2)]
        rstd2 = [sb(f"rstd2{i}", [P, 1]) for i in range(2)]
        y = [sb(f"y{i}", [P, N]) for i in range(2)]
        yt_hi = [sb(f"yt_hi{i}", [P, N], F32R) for i in range(2)]
        yt_lo = [sb(f"yt_lo{i}", [P, N], F32R) for i in range(2)]
        result = [sb(f"result{i}", [P, N]) for i in range(2)]

        score_bank = [bank(f"score_bank{i}") for i in range(SBANKS)]
        turn_bank = [bank(f"turn_bank{i}") for i in range(2)]
        pv_bank = bank("pv_bank")
        proj_bank = bank("proj_bank")

        w_loaded = sem("w_loaded")
        b_loaded = sem("b_loaded")
        first_loaded = [sem(f"first_loaded{i}") for i in range(3)]
        tile_loaded = sem("tile_loaded")
        ffn_w_loaded = sem("ffn_w_loaded")
        ctx_now_loaded = sem("ctx_now_loaded")
        stacked = [sem(f"stacked{b}") for b in range(2)]
        stored = [sem(f"stored{i}") for i in range(2)]
        zeroed = sem("zeroed")
        consts_ready = sem("consts_ready")
        ident_zeroed = sem("ident_zeroed")
        ident_ready = sem("ident_ready")
        w_hi_ready = sem("w_hi_ready")
        w_split = sem("w_split")
        gates_ready = sem("gates_ready")
        stats_done = sem("stats_done")
        mean_var_done = sem("mean_var_done")
        var_eps_done = sem("var_eps_done")
        rstd_done = sem("rstd_done")
        xn_done = sem("xn_done")
        ctxn_done = sem("ctxn_done")
        x_hi_done = sem("x_hi_done")
        c_hi_done = sem("c_hi_done")
        x_lo_done = sem("x_lo_done")
        c_lo_done = sem("c_lo_done")
        q_done = sem("q_done")
        k_done = sem("k_done")
        q_hi_done = sem("q_hi_done")
        k_hi_done = sem("k_hi_done")
        q_lo_done = sem("q_lo_done")
        k_lo_done = sem("k_lo_done")
        s_done = sem("s_done")
        s_kept = sem("s_kept")
        s_squared = sem("s_squared")
        scores_done = sem("scores_done")
        max_done = sem("max_done")
        exp_done = sem("exp_done")
        rden_done = sem("rden_done")
        probs_done = sem("probs_done")
        turned = sem("turned")
        turned_kept = sem("turned_kept")
        pv_done = sem("pv_done")
        mean_squared = sem("mean_squared")
        var_done = sem("var_done")
        xm_done = sem("xm_done")
        relu_done = sem("relu_done")
        w_scaled = sem("w_scaled")
        w_deq_done = sem("w_deq_done")
        ffn_hi_done = sem("ffn_hi_done")
        ffn_lo_done = sem("ffn_lo_done")
        root_done = sem("root_done")
        scaled_done = sem("scaled_done")
        x2_done = sem("x2_done")
        stats2_done = sem("stats2_done")
        mean_var2_done = sem("mean_var2_done")
        var_eps2_done = sem("var_eps2_done")
        rstd2_done = sem("rstd2_done")
        y_done = sem("y_done")
        y_turned = sem("y_turned")
        yt_hi_done = sem("yt_hi_done")
        yt_lo_done = sem("yt_lo_done")
        ffn_done = sem("ffn_done")
        result_done = sem("result_done")

        def tile_of(tensor, t):
            if isinstance(t, int):
                return tensor[:, t, :]
            return tensor[:, bass.ds(t, 1), :].rearrange("p a n -> p (a n)")

        def half_of(tensor, t, b):
            if isinstance(t, int):
                return tensor[C * b:C * b + C, t, :]
            return tensor[C * b:C * b + C, bass.ds(t, 1), :].rearrange("p a n -> p (a n)")

        def dram_tile(ap, t):
            if isinstance(t, int):
                return ap[t]
            return ap[bass.ds(t, 1)].rearrange("a p n -> p (a n)")

        def held(eng, count):
            return count if isinstance(count, int) else eng.to_reg(count)

        def over_tiles(eng, body):
            body(0)
            with eng.Fori(1, TILES - 2) as t:
                body(t)
            body(TILES - 2)
            body(TILES - 1)

        def is_first(t):
            return isinstance(t, int) and t == 0

        def has_next(t):
            return not isinstance(t, int) or t + 1 < TILES

        def has_second_next(t):
            return not isinstance(t, int) or t + 2 < TILES

        block = ctx.enter_context(nc.Block())

        @block.sync
        def _(sp):
            def load(t, done):
                sp.dma_start(tile_of(X, t), dram_tile(x_tiles, t)).then_inc(done, DMA)
                sp.dma_start(tile_of(CTX, t), dram_tile(context_tiles, t)).then_inc(done, DMA)

            def stack(t, b):
                rows = slice(C * b, C * b + C)
                for dst, up, down in ((q_stack[b], q_hi, q_lo), (k_same[b], k_hi, k_lo),
                                      (k_cross[b], k_lo, k_hi)):
                    sp.dma_start(dst[0:C, :].bitcast(F32), up[rows, :].bitcast(F32)).then_inc(stacked[b], DMA)
                    sp.dma_start(dst[C:P, :].bitcast(F32), down[rows, :].bitcast(F32)).then_inc(stacked[b], DMA)

            load(0, first_loaded[0])
            sp.wait_ge(zeroed, 2)
            for h in range(2):
                rows = slice(C * h, C * h + C)
                sp.dma_start(w_qk[rows, 0, rows], wq_t).then_inc(w_loaded, DMA)
                sp.dma_start(w_qk[rows, 1, rows], wk_t).then_inc(w_loaded, DMA)
                sp.dma_start(w_s[rows, rows], ws_t).then_inc(w_loaded, DMA)
                sp.dma_start(b_qk[rows, 0:1], bq.rearrange("(c a) -> c a", a=1)).then_inc(b_loaded, DMA)
                sp.dma_start(b_qk[rows, 1:2], bk.rearrange("(c a) -> c a", a=1)).then_inc(b_loaded, DMA)
            sp.dma_start(b_s[:, :], bs.partition_broadcast(P)).then_inc(b_loaded, DMA)
            sp.dma_start(gates[:, 0:1], g_xattn.partition_broadcast(P)).then_inc(b_loaded, DMA)
            sp.dma_start(gates[:, 1:2], g_ffn.partition_broadcast(P)).then_inc(b_loaded, DMA)
            load(1, first_loaded[1])
            sp.wait_ge(q_lo_done, 1)
            sp.wait_ge(k_lo_done, 1)
            stack(0, 0)
            stack(0, 1)
            load(2, first_loaded[2])
            sp.dma_start(ctx_now[:, :], dram_tile(context_tiles, 0)).then_inc(ctx_now_loaded, DMA)
            sp.dma_start(w_int[:, :, :], weight_q_t.rearrange("(g p) o -> p g o", p=P)).then_inc(ffn_w_loaded, DMA)
            for g in range(GROUPS):
                sp.dma_start(sz[:, g, :, :], scales_zeros[g].partition_broadcast(P)).then_inc(ffn_w_loaded, DMA)

            def body(t):
                if not has_next(t):
                    return
                sp.wait_ge(q_lo_done, t + 2)
                sp.wait_ge(k_lo_done, t + 2)
                sp.wait_ge(scores_done, CHUNKS * t + JC)
                stack(t + 1, 0)
                sp.wait_ge(s_done, t + 1)
                sp.dma_start(ctx_now[:, :], dram_tile(context_tiles, t + 1)).then_inc(ctx_now_loaded, DMA)
                sp.wait_ge(scores_done, CHUNKS * t + CHUNKS)
                stack(t + 1, 1)

            body(0)
            load(3, tile_loaded)
            with sp.Fori(1, TILES - 4) as t:
                body(t)
                sp.wait_ge(tile_loaded, 2 * DMA * t)
                load(t + 3, tile_loaded)
            for t in range(TILES - 4, TILES):
                body(t)
                if t + 3 < TILES:
                    sp.wait_ge(tile_loaded, 2 * DMA * t)
                    load(t + 3, tile_loaded)

            sp.wait_ge(result_done, 1)
            sp.dma_start(dram_tile(out_tiles, 0), result[0][:, :]).then_inc(stored[0], DMA)
            sp.wait_ge(result_done, 2)
            sp.dma_start(dram_tile(out_tiles, 1), result[1][:, :]).then_inc(stored[1], DMA)
            with sp.Fori(2, TILES - 1, 2) as u:
                for i in range(2):
                    sp.wait_ge(result_done, u + i + 1)
                    sp.dma_start(dram_tile(out_tiles, u + i), result[i][:, :]).then_inc(stored[i], DMA)
            for i in range(2):
                sp.wait_ge(stored[i], DMA * TILES // 2)

        @block.tensor
        def _(pe):
            def project(t, which):
                hi, lo, hi_done, lo_done, done = (
                    (x_hi, x_lo, x_hi_done, x_lo_done, q_done), (c_hi, c_lo, c_hi_done, c_lo_done, k_done))[which]
                pe.wait_ge(hi_done, t + 1)
                pe.wait_ge(lo_done, t + 1)
                pe.matmul(proj_bank[:, :], w_qk_hi[:, which, :], hi[:, :], start=True, stop=False)
                pe.matmul(proj_bank[:, :], w_qk_hi[:, which, :], lo[:, :], start=False, stop=False)
                pe.matmul(proj_bank[:, :], w_qk_lo[:, which, :], hi[:, :], start=False, stop=True).then_inc(done, 1)

            def scores(t, c):
                b, j = c // JC, c % JC
                if j == 0:
                    pe.wait_ge(stacked[b], STACK * (t + 1))
                if not (is_first(t) and c < SBANKS):
                    pe.wait_ge(exp_done, CHUNKS * t + c - SBANKS + 1)
                q_part = q_stack[b][:, P * j:P * j + P]
                pe.matmul(score_bank[c % SBANKS][:, :], q_part, k_same[b][:, :], start=True, stop=False)
                pe.matmul(score_bank[c % SBANKS][:, :], q_part, k_cross[b][:, :],
                          start=False, stop=True).then_inc(scores_done, 1)

            def turn(t, c):
                pe.wait_ge(probs_done, CHUNKS * t + c + 1)
                if not (is_first(t) and c < 2):
                    pe.wait_ge(turned_kept, CHUNKS * t + c - 1)
                for i in range(JC):
                    last = pe.transpose(turn_bank[c % 2][:, P * i:P * i + P],
                                        probs[c % SBANKS][:, P * i:P * i + P], ident[:, :])
                last.then_inc(turned, 1)

            def weigh(t, b, i):
                if i == 0:
                    pe.wait_ge(turned_kept, CHUNKS * t + JC * b + JC)
                    pe.wait_ge(s_squared, t + 1)
                    if not (is_first(t) and b == 0):
                        pe.wait_ge(var_done, 2 * t + b)
                        pe.wait_ge(xm_done, 2 * t + b)
                mm = pe.matmul(pv_bank[:, :], values[:, i, b, :, :].rearrange("p a c -> p (a c)"),
                               probs_t[b][:, i, :], start=(i == 0), stop=(i == JC - 1))
                if i == JC - 1:
                    mm.then_inc(pv_done, 1)

            def value_product(t):
                pe.wait_ge(ctx_now_loaded, DMA * (t + 1))
                k_tile = t + 1 if has_next(t) else t
                pe.wait_ge(k_hi_done, k_tile + 1)
                pe.wait_ge(k_lo_done, k_tile + 1)
                for i in range(JC):
                    last = pe.matmul(proj_bank[:, P * i:P * i + P], ctx_now[:, P * i:P * i + P], w_s[:, :],
                                     start=True, stop=True)
                last.then_inc(s_done, 1)

            pe.wait_ge(w_split, 1)
            pe.wait_ge(w_loaded, 6 * DMA)
            project(0, 0)
            pe.wait_ge(q_hi_done, 1)
            pe.wait_ge(q_lo_done, 1)
            project(0, 1)
            for c in range(AHEAD_S):
                scores(0, c)
            pe.wait_ge(ident_ready, 1)

            def body(t):
                for c in range(CHUNKS):
                    if c + AHEAD_S < CHUNKS:
                        scores(t, c + AHEAD_S)
                    elif has_next(t):
                        scores(t + 1, c + AHEAD_S - CHUNKS)
                    if c == 0 and has_next(t):
                        if not is_first(t):
                            pe.wait_ge(s_kept, t)
                        else:
                            pe.wait_ge(k_hi_done, 1)
                            pe.wait_ge(k_lo_done, 1)
                        project(t + 1, 0)
                    if c == 2 and has_next(t):
                        pe.wait_ge(q_hi_done, t + 2)
                        pe.wait_ge(q_lo_done, t + 2)
                        project(t + 1, 1)
                    turn(t, c)
                    if 1 <= c <= 3 and not is_first(t):
                        for i in ((0, 1), (2,), (3,))[c - 1]:
                            weigh(t - 1, 1, i)
                    if c == 3:
                        value_product(t)
                    if 5 <= c <= 7:
                        for i in ((0, 1), (2,), (3,))[c - 5]:
                            weigh(t, 0, i)

            over_tiles(pe, body)
            for i in range(JC):
                weigh(TILES - 1, 1, i)

            def turn_y(u, i):
                pe.wait_ge(y_done, u + 1)
                if not (isinstance(u, int) and u < 2):
                    pe.wait_ge(yt_lo_done, u - 1)
                for g in range(GROUPS):
                    last = pe.transpose(score_bank[i][:, P * g:P * g + P], y[i][:, P * g:P * g + P], ident[:, :])
                last.then_inc(y_turned, 1)

            def feed_forward(u, i):
                pe.wait_ge(yt_hi_done, u + 1)
                pe.wait_ge(yt_lo_done, u + 1)
                if not (isinstance(u, int) and u < 2):
                    pe.wait_ge(result_done, u - 1)
                for g in range(GROUPS):
                    hi, lo = (a[i][:, P * g:P * g + P] for a in (yt_hi, yt_lo))
                    pe.matmul(score_bank[2 + i][:, :], hi, w_hi[:, g, :], start=(g == 0), stop=False)
                    pe.matmul(score_bank[2 + i][:, :], hi, w_lo[:, g, :], start=False, stop=False)
                    mm = pe.matmul(score_bank[2 + i][:, :], lo, w_hi[:, g, :], start=False,
                                   stop=(g == GROUPS - 1))
                mm.then_inc(ffn_done, 1)

            pe.wait_ge(exp_done, LAST)
            turn_y(0, 0)
            turn_y(1, 1)
            pe.wait_ge(ffn_hi_done, GROUPS)
            pe.wait_ge(ffn_lo_done, GROUPS)
            feed_forward(0, 0)

            def pair(u):
                turn_y(u, 0)
                feed_forward(u - 1, 1)
                turn_y(u + 1, 1)
                feed_forward(u, 0)

            pair(2)
            with pe.Fori(4, TILES - 1, 2) as u:
                pair(u)
            feed_forward(TILES - 1, 1)

        @block.scalar
        def _(act):
            def keep_hi(t, which):
                if which == 0:
                    act.wait_ge(q_done, t + 1)
                    if not is_first(t):
                        act.wait_ge(stacked[0], STACK * t)
                        act.wait_ge(stacked[1], STACK * t)
                    act.activation(q_hi[:, :], proj_bank[:, :], ACT.Identity,
                                   bias=b_qk[:, 0:1]).then_inc(q_hi_done, 1)
                else:
                    act.wait_ge(k_done, t + 1)
                    act.activation(k_hi[:, :], proj_bank[:, :], ACT.Identity,
                                   bias=b_qk[:, 1:2]).then_inc(k_hi_done, 1)

            def exponentials(t, c):
                act.wait_ge(max_done, CHUNKS * t + c + 1)
                if not (is_first(t) and c < SBANKS):
                    act.wait_ge(turned, CHUNKS * t + c - SBANKS + 1)
                act.activation(probs[c % SBANKS][:, :], score_bank[c % SBANKS][:, :], ACT.Exp,
                               bias=neg_max[:, c:c + 1], accum_out=den[:, c:c + 1]).then_inc(exp_done, 1)

            def keep_turned(t, c):
                b, j = c // JC, c % JC
                act.wait_ge(turned, CHUNKS * t + c + 1)
                if j == 0 and not is_first(t):
                    act.wait_ge(pv_done, 2 * t + b - 1)
                act.copy(probs_t[b][:, :, P * j:P * j + P],
                         turn_bank[c % 2][:, :].rearrange("p (i n) -> p i n", i=JC)).then_inc(turned_kept, 1)

            def square_mean(t, b):
                act.wait_ge(pv_done, 2 * t + b + 1)
                if not (is_first(t) and b == 0):
                    act.wait_ge(var_done, 2 * t + b)
                act.activation(mean_sq[C:P, :], pv_bank[0:C, :], ACT.Square).then_inc(mean_squared, 1)

            act.wait_ge(b_loaded, 7 * DMA)
            act.activation(tanh_g[:, :], gates[:, :], ACT.Tanh).then_inc(gates_ready, 1)
            keep_hi(0, 0)
            keep_hi(0, 1)
            for c in range(AHEAD_E):
                exponentials(0, c)

            def body(t):
                for c in range(CHUNKS):
                    if c + AHEAD_E < CHUNKS:
                        exponentials(t, c + AHEAD_E)
                    elif has_next(t):
                        exponentials(t + 1, c + AHEAD_E - CHUNKS)
                    if c == 0 and not is_first(t):
                        square_mean(t - 1, 0)
                    if c == 4 and not is_first(t):
                        square_mean(t - 1, 1)
                    if c > 0:
                        keep_turned(t, c - 1)
                    elif not is_first(t):
                        keep_turned(t - 1, CHUNKS - 1)
                    if c == 0 and has_next(t):
                        keep_hi(t + 1, 0)
                    if c == 2 and has_next(t):
                        keep_hi(t + 1, 1)

            over_tiles(act, body)
            square_mean(TILES - 1, 0)
            keep_turned(TILES - 1, CHUNKS - 1)
            square_mean(TILES - 1, 1)

            def root(u):
                act.wait_ge(relu_done, u + 1)
                act.activation(tile_of(VAR, u), tile_of(VAR, u), ACT.Sqrt).then_inc(root_done, 1)

            def keep_y_hi(u, i):
                act.wait_ge(y_turned, u + 1)
                if not (isinstance(u, int) and u < 2):
                    act.wait_ge(ffn_done, u - 1)
                act.copy(yt_hi[i][:, :], score_bank[i][:, :]).then_inc(yt_hi_done, 1)


            def pair(u):
                root(u)
                keep_y_hi(u - 2, 0)
                root(u + 1)
                keep_y_hi(u - 1, 1)

            root(0)
            root(1)
            pair(2)
            with act.Fori(4, TILES - 1, 2) as u:
                pair(u)
            keep_y_hi(TILES - 2, 0)
            keep_y_hi(TILES - 1, 1)

        @block.vector
        def _(dve):
            def statistics(t, loaded, count):
                count = held(dve, count)
                dve.wait_ge(zeroed, 1)
                dve.wait_ge(loaded, count)
                dve.bn_stats(stats[:, 0, :], tile_of(X, t))
                dve.bn_stats(stats[:, 1, :], tile_of(CTX, t)).then_inc(stats_done, 1)
                count = held(dve, t + 1)
                dve.wait_ge(zeroed, 1)
                dve.wait_ge(stats_done, count)
                dve.bn_aggr(mean_var[:, 0, :], stats[:, 0, :])
                dve.bn_aggr(mean_var[:, 1, :], stats[:, 1, :]).then_inc(mean_var_done, 1)
                dve.wait_ge(mean_var_done, t + 1)
                dve.tensor_scalar(var_eps[:, 0:1], mean_var[:, 0, 1:2], 1.0 + EPS, EPS * EPS, ALU.mult, ALU.add)
                dve.tensor_scalar(var_eps[:, 1:2], mean_var[:, 1, 1:2], EPS, None,
                                  ALU.add).then_inc(var_eps_done, 1)

            def normalise(t):
                dve.wait_ge(rstd_done, t + 1)
                if not is_first(t):
                    dve.wait_ge(x_lo_done, t)
                    dve.wait_ge(q_done, t)
                    dve.wait_ge(k_done, t)
                dve.tensor_scalar(xn[:, :], tile_of(X, t), mean_var[:, 0, 0:1], rstd[:, 0:1],
                                  ALU.subtract, ALU.mult).then_inc(xn_done, 1)
                dve.tensor_scalar(tile_of(CTX, t), tile_of(CTX, t), mean_var[:, 1, 0:1], rstd[:, 1:2],
                                  ALU.subtract, ALU.mult).then_inc(ctxn_done, 1)
                dve.wait_ge(xn_done, t + 1)
                dve.tensor_copy(x_hi[:, :], xn[:, :]).then_inc(x_hi_done, 1)
                count = held(dve, t + 1)
                dve.wait_ge(zeroed, 1)
                dve.wait_ge(ctxn_done, count)
                dve.tensor_copy(c_hi[:, :], tile_of(CTX, t)).then_inc(c_hi_done, 1)

            def keep_lo(t, which):
                hi, lo, hi_done, lo_done = ((q_hi, q_lo, q_hi_done, q_lo_done),
                                            (k_hi, k_lo, k_hi_done, k_lo_done))[which]
                dve.wait_ge(hi_done, t + 1)
                dve.scalar_tensor_tensor(lo[:, :], proj_bank[:, :], b_qk[:, which:which + 1],
                                         hi[:, :].bitcast(F32), ALU.add, ALU.subtract).then_inc(lo_done, 1)

            def maximum(t, c):
                dve.wait_ge(scores_done, CHUNKS * t + c + 1)
                dve.tensor_reduce(neg_max[:, c:c + 1], score_bank[c % SBANKS][:, :], AX_X, ALU.max,
                                  negate=True).then_inc(max_done, 1)

            def reciprocal(t, c):
                dve.wait_ge(exp_done, CHUNKS * t + c + 1)
                dve.reciprocal(rden[:, c:c + 1], den[:, c:c + 1]).then_inc(rden_done, 1)

            def variance(t, b):
                dve.wait_ge(mean_squared, 2 * t + b + 1)
                dve.tensor_tensor(half_of(VAR, t, b), pv_bank[C:P, :], mean_sq[C:P, :],
                                  ALU.subtract).then_inc(var_done, 1)
                dve.scalar_tensor_tensor(half_of(XM, t, b), pv_bank[0:C, :], tanh_g[0:C, 0:1],
                                         half_of(X, t, b), ALU.mult, ALU.add).then_inc(xm_done, 1)

            def relu(t):
                dve.wait_ge(var_done, 2 * t + 2)
                dve.tensor_scalar(tile_of(VAR, t), tile_of(VAR, t), 0.0, None, ALU.max).then_inc(relu_done, 1)

            def keep_values(t):
                dve.wait_ge(s_done, t + 1)
                if not is_first(t):
                    dve.wait_ge(pv_done, 2 * t)
                dve.tensor_tensor(values[:, :, :, 0, :].rearrange("p i b c -> p (i b) c"),
                                  proj_bank[:, :].rearrange("p (i c) -> p i c", c=C),
                                  b_s[:, :].unsqueeze(1).broadcast_to([P, 2 * JC, C]),
                                  ALU.add).then_inc(s_kept, 1)

            def scale_weights(g):
                if g >= 2:
                    dve.wait_ge(ffn_lo_done, g - 1)
                else:
                    dve.wait_ge(ffn_w_loaded, (1 + GROUPS) * DMA)
                dve.scalar_tensor_tensor(w_deq[g % 2][:, :], w_int[:, g, :], -QUANT_ZERO, sz[:, g, 0, :],
                                         ALU.add, ALU.mult).then_inc(w_scaled, 1)

            def weights_hi(g):
                dve.wait_ge(w_deq_done, g + 1)
                dve.tensor_copy(w_hi[:, g, :], w_deq[g % 2][:, :]).then_inc(ffn_hi_done, 1)

            statistics(0, first_loaded[0], 2 * DMA)
            dve.wait_ge(w_loaded, 6 * DMA)
            dve.tensor_copy(w_qk_hi[:, :, :], w_qk[:, :, :]).then_inc(w_hi_ready, 1)
            dve.wait_ge(w_hi_ready, 1)
            dve.tensor_tensor(w_qk_lo[:, :, :], w_qk[:, :, :], w_qk_hi[:, :, :].bitcast(F32),
                              ALU.subtract).then_inc(w_split, 1)
            normalise(0)
            dve.wait_ge(b_loaded, 7 * DMA)
            keep_lo(0, 0)
            keep_lo(0, 1)
            statistics(1, first_loaded[1], 2 * DMA)
            normalise(1)
            dve.wait_ge(gates_ready, 1)
            for c in range(AHEAD_S):
                maximum(0, c)
                if c > 0:
                    reciprocal(0, c - 1)

            def body(t):
                for c in range(CHUNKS):
                    if c + AHEAD_S < CHUNKS:
                        maximum(t, c + AHEAD_S)
                    elif has_next(t):
                        maximum(t + 1, c + AHEAD_S - CHUNKS)
                    if c + AHEAD_E < CHUNKS:
                        reciprocal(t, c + AHEAD_E)
                    elif has_next(t):
                        reciprocal(t + 1, c + AHEAD_E - CHUNKS)
                    if c == 0 and not is_first(t):
                        variance(t - 1, 0)
                    if c == 1 and has_next(t):
                        keep_lo(t + 1, 0)
                    if c == 3 and has_next(t):
                        keep_lo(t + 1, 1)
                    if c == 4:
                        if not is_first(t):
                            variance(t - 1, 1)
                        keep_values(t)
                        if not is_first(t):
                            relu(t - 1)
                    if has_second_next(t):
                        if c == 5:
                            if is_first(t):
                                statistics(2, first_loaded[2], 2 * DMA)
                            else:
                                statistics(t + 2, tile_loaded, 2 * DMA * t)
                        if c == 7:
                            normalise(t + 2)
                    else:
                        g = (t - TILES + 2) * (GROUPS // 2)
                        if c == 1:
                            scale_weights(g)
                        if c == 2:
                            weights_hi(g)
                        if c == 5:
                            scale_weights(g + 1)
                        if c == 6:
                            weights_hi(g + 1)

            over_tiles(dve, body)
            variance(TILES - 1, 0)
            variance(TILES - 1, 1)
            relu(TILES - 1)

            def after_attention(u, i):
                dve.wait_ge(scaled_done, u + 1)
                dve.scalar_tensor_tensor(tile_of(X, u), scaled[i][:, :], tanh_g[:, 0:1], tile_of(XM, u),
                                         ALU.mult, ALU.add).then_inc(x2_done, 1)
                count = held(dve, u + 1)
                dve.wait_ge(zeroed, 1)
                dve.wait_ge(x2_done, count)
                dve.bn_stats(stats2[i][:, :], tile_of(X, u)).then_inc(stats2_done, 1)
                count = held(dve, u + 1)
                dve.wait_ge(zeroed, 1)
                dve.wait_ge(stats2_done, count)
                dve.bn_aggr(mean_var2[i][:, :], stats2[i][:, :]).then_inc(mean_var2_done, 1)
                dve.wait_ge(mean_var2_done, u + 1)
                dve.tensor_scalar(var_eps2[i][:, :], mean_var2[i][:, 1:2], EPS, None,
                                  ALU.add).then_inc(var_eps2_done, 1)

            def normalise_y(u, i):
                dve.wait_ge(rstd2_done, u + 1)
                if not (isinstance(u, int) and u < 2):
                    dve.wait_ge(y_turned, u - 1)
                dve.tensor_scalar(y[i][:, :], tile_of(X, u), mean_var2[i][:, 0:1], rstd2[i][:, :],
                                  ALU.subtract, ALU.mult).then_inc(y_done, 1)

            def keep_y_lo(u, i):
                dve.wait_ge(yt_hi_done, u + 1)
                dve.tensor_tensor(yt_lo[i][:, :], score_bank[i][:, :], yt_hi[i][:, :].bitcast(F32),
                                  ALU.subtract).then_inc(yt_lo_done, 1)

            def add_ffn(u, i):
                dve.wait_ge(ffn_done, u + 1)
                if not (isinstance(u, int) and u < 2):
                    dve.wait_ge(stored[i], DMA // 2 * (u - i))
                dve.scalar_tensor_tensor(result[i][:, :], score_bank[2 + i][:, :], tanh_g[:, 1:2],
                                         tile_of(X, u), ALU.mult, ALU.add).then_inc(result_done, 1)

            after_attention(0, 0)
            after_attention(1, 1)
            normalise_y(0, 0)
            normalise_y(1, 1)
            keep_y_lo(0, 0)
            keep_y_lo(1, 1)
            after_attention(2, 0)
            after_attention(3, 1)
            normalise_y(2, 0)
            normalise_y(3, 1)
            add_ffn(0, 0)
            add_ffn(1, 1)
            with dve.Fori(2, TILES - 3, 2) as u:
                for i in range(2):
                    keep_y_lo(u + i, i)
                    after_attention(u + i + 2, i)
                    normalise_y(u + i + 2, i)
                    add_ffn(u + i, i)
            for i in range(2):
                keep_y_lo(TILES - 2 + i, i)
                add_ffn(TILES - 2 + i, i)

        @block.gpsimd
        def _(pool):
            def inverse_deviation(t):
                pool.wait_ge(var_eps_done, t + 1)
                pool.tensor_tensor(rstd[:, :], var_eps[:, :], power[:, :], ALU.pow).then_inc(rstd_done, 1)

            def split_lo(t):
                pool.wait_ge(x_hi_done, t + 1)
                if not is_first(t):
                    pool.wait_ge(q_done, t)
                pool.tensor_tensor(x_lo[:, :], xn[:, :], x_hi[:, :].bitcast(F32),
                                   ALU.subtract).then_inc(x_lo_done, 1)
                pool.wait_ge(c_hi_done, t + 1)
                if not is_first(t):
                    pool.wait_ge(k_done, t)
                pool.tensor_tensor(c_lo[:, :], tile_of(CTX, t), c_hi[:, :].bitcast(F32),
                                   ALU.subtract).then_inc(c_lo_done, 1)

            def normalise_probs(t, c):
                count = held(pool, CHUNKS * t + c + 1)
                pool.wait_ge(ident_ready, 1)
                pool.wait_ge(rden_done, count)
                pool.tensor_scalar(probs[c % SBANKS][:, :], probs[c % SBANKS][:, :], rden[:, c:c + 1], 1.0,
                                   ALU.mult, ALU.mult).then_inc(probs_done, 1)

            def square_values(t):
                pool.wait_ge(s_kept, t + 1)
                kept = values[:, :, :, 0, :].rearrange("p i b c -> p (i b) c")
                squared = values[:, :, :, 1, :].rearrange("p i b c -> p (i b) c")
                pool.tensor_tensor(squared, kept, kept, ALU.mult).then_inc(s_squared, 1)

            def dequantise(g):
                pool.wait_ge(w_scaled, g + 1)
                pool.tensor_tensor(w_deq[g % 2][:, :], w_deq[g % 2][:, :], sz[:, g, 1, :],
                                   ALU.add).then_inc(w_deq_done, 1)

            def weights_lo(g):
                pool.wait_ge(ffn_hi_done, g + 1)
                pool.tensor_tensor(w_lo[:, g, :], w_deq[g % 2][:, :], w_hi[:, g, :].bitcast(F32),
                                   ALU.subtract).then_inc(ffn_lo_done, 1)

            pool.memset(w_qk[:, :, :], 0.0).then_inc(zeroed, 1)
            pool.memset(w_s[:, :], 0.0).then_inc(zeroed, 1)
            pool.memset(ident[:, :], 0.0).then_inc(ident_zeroed, 1)
            pool.memset(power[:, :], -0.5).then_inc(consts_ready, 1)
            pool.wait_ge(ident_zeroed, 1)
            pool.affine_select(out=ident[:, :], in_=ident[:, :], compare_op=ALU.not_equal, fill=1.0, base=0,
                               pattern=[[-1, P]], channel_multiplier=1).then_inc(ident_ready, 1)
            pool.wait_ge(consts_ready, 1)
            inverse_deviation(0)
            split_lo(0)
            inverse_deviation(1)
            split_lo(1)
            for c in range(AHEAD_E):
                normalise_probs(0, c)

            def body(t):
                for c in range(CHUNKS):
                    if c + AHEAD_E < CHUNKS:
                        normalise_probs(t, c + AHEAD_E)
                    elif has_next(t):
                        normalise_probs(t + 1, c + AHEAD_E - CHUNKS)
                    if c == 4:
                        square_values(t)
                    if has_second_next(t):
                        if c == 6:
                            inverse_deviation(t + 2)
                        if c == 7:
                            split_lo(t + 2)
                    else:
                        g = (t - TILES + 2) * (GROUPS // 2)
                        if c == 1:
                            dequantise(g)
                        if c == 2:
                            weights_lo(g)
                        if c == 5:
                            dequantise(g + 1)
                        if c == 6:
                            weights_lo(g + 1)

            over_tiles(pool, body)

            def scale_context(u, i):
                pool.wait_ge(root_done, u + 1)
                if not (isinstance(u, int) and u < 2):
                    pool.wait_ge(x2_done, u - 1)
                pool.tensor_tensor(scaled[i][:, :], tile_of(CTX, u), tile_of(VAR, u),
                                   ALU.mult).then_inc(scaled_done, 1)

            def inverse_deviation2(u, i):
                pool.wait_ge(var_eps2_done, u + 1)
                if not (isinstance(u, int) and u < 2):
                    pool.wait_ge(y_done, u - 1)
                pool.tensor_tensor(rstd2[i][:, :], var_eps2[i][:, :], power[:, 0:1],
                                   ALU.pow).then_inc(rstd2_done, 1)

            scale_context(0, 0)
            scale_context(1, 1)
            inverse_deviation2(0, 0)
            inverse_deviation2(1, 1)
            with pool.Fori(2, TILES - 1, 2) as u:
                for i in range(2):
                    scale_context(u + i, i)
                for i in range(2):
                    inverse_deviation2(u + i, i)


def kernel(**inputs):
    import numpy as np
    import concourse.bacc as bacc
    from concourse.bass_utils import run_bass_kernel_spmd as run

    def laid(name, order=None):
        a = np.asarray(inputs[name])
        return np.ascontiguousarray(a if order is None else a.transpose(order))

    arrays = {
        "x": laid("x"),
        "context": laid("ctx_4096"),
        "g_xattn": laid("g_xattn"),
        "g_ffn": laid("g_ffn"),
        "wq_t": laid("L0_xattn_Wq", (1, 0)),
        "bq": laid("L0_xattn_bq"),
        "wk_t": laid("L0_xattn_Wk", (1, 0)),
        "bk": laid("L0_xattn_bk"),
        "ws_t": laid("L0_xattn_Ws", (1, 0)),
        "bs": laid("L0_xattn_bs_"),
        "weight_q_t": laid("L0_ffn_weight_q", (1, 0)),
        "scales_zeros": laid("L0_ffn_scales_and_zeros", (0, 2, 1)),
    }
    nc = bacc.Bacc("TRN2", target_bir_lowering=False, num_devices=1)
    args = [nc.dram_tensor(f"in_{n}", a.shape, mybir.dt.from_np(a.dtype), kind="ExternalInput").ap()
            for n, a in arrays.items()]
    out = nc.dram_tensor("out_0", arrays["x"].shape, F32, kind="ExternalOutput").ap()
    gated_attention_ffn(nc, *args, out)
    r = run(nc, [{f"in_{n}": a for n, a in arrays.items()}], core_ids=[0])
    return r.results[0]["out_0"]
```

```python
from contextlib import ExitStack

import concourse.bass as bass
from concourse import mybir

F32 = mybir.dt.float32
F32R = mybir.dt.float32r
I32 = mybir.dt.int32
ALU = mybir.AluOpType
ACT = mybir.ActivationFunctionType
AX_X = mybir.AxisListType.X

EPS = 1e-5
QUANT_ZERO = 8.0
P = 128


def gated_attention_ffn(nc, x, context, params, weight_q_t, scales_zeros, out):
    BATCHES, C, N = x.shape
    TILES = BATCHES // 2
    JC = N // P
    CHUNKS = 2 * JC
    GROUPS = weight_q_t.shape[0] // P
    AHEAD_S, AHEAD_E = 3, 2
    SBANKS = 4
    LAST = CHUNKS * TILES
    DMA = 16
    STACK = 6 * DMA
    assert 2 * C == P and N == 512 and CHUNKS % SBANKS == 0

    x_tiles = x.rearrange("(t b) c n -> t (b c) n", b=2)
    context_tiles = context.rearrange("(t b) c n -> t (b c) n", b=2)
    out_tiles = out.rearrange("(t b) c n -> t (b c) n", b=2)

    with ExitStack() as ctx:
        def sb(name, shape, dt=F32):
            return ctx.enter_context(nc.sbuf_tensor(name, shape, dt))

        def bank(name):
            return ctx.enter_context(nc.psum_tensor(name, [P, 512], F32))

        def sem(name):
            return ctx.enter_context(nc.semaphore(name))

        X = sb("X", [P, TILES, N])
        CTX = sb("CTX", [P, TILES, N])
        MEAN = sb("MEAN", [P, TILES, N])
        VAR = sb("VAR", [P, TILES, N])
        params_sb = sb("params_sb", [P, params.shape[1]])
        w_qk = params_sb[:, 0:2 * P].rearrange("p (w o) -> p w o", w=2)
        w_s = params_sb[:, 2 * P:3 * P]
        b_qk = params_sb[:, 3 * P:3 * P + 2]
        gates = params_sb[:, 3 * P + 2:3 * P + 4]
        b_s = params_sb[:, 3 * P + 4:3 * P + 4 + C]
        w_qk_hi = sb("w_qk_hi", [P, 2, P], F32R)
        w_qk_lo = sb("w_qk_lo", [P, 2, P], F32R)
        xn = sb("xn", [P, N])
        x_hi = sb("x_hi", [P, N], F32R)
        x_lo = sb("x_lo", [P, N], F32R)
        c_hi = sb("c_hi", [P, N], F32R)
        c_lo = sb("c_lo", [P, N], F32R)
        ctx_now = sb("ctx_now", [P, N])
        stats = sb("stats", [P, 2, 6])
        mean_var = sb("mean_var", [P, 2, 2])
        var_eps = sb("var_eps", [P, 2])
        rstd = sb("rstd", [P, 2])
        q_hi = sb("q_hi", [P, N], F32R)
        q_lo = sb("q_lo", [P, N], F32R)
        k_hi = sb("k_hi", [P, N], F32R)
        k_lo = sb("k_lo", [P, N], F32R)
        q_stack = [sb(f"q_stack{b}", [P, N], F32R) for b in range(2)]
        k_same = [sb(f"k_same{b}", [P, N], F32R) for b in range(2)]
        k_cross = [sb(f"k_cross{b}", [P, N], F32R) for b in range(2)]
        probs = [sb(f"probs{i}", [P, N]) for i in range(SBANKS)]
        neg_max = sb("neg_max", [P, CHUNKS])
        den = sb("den", [P, CHUNKS])
        rden = sb("rden", [P, CHUNKS])
        probs_t = [sb(f"probs_t{b}", [P, JC, N]) for b in range(2)]
        values = sb("values", [P, JC, 2, 2, C])
        mean_sq = sb("mean_sq", [P, N])
        ident = sb("ident", [P, P])
        power = sb("power", [P, 2])
        tanh_g = sb("tanh_g", [P, 2])
        w_int = sb("w_int", [P, GROUPS, N], I32)
        sz = sb("sz", [P, GROUPS, 2, N])
        w_deq = [sb(f"w_deq{i}", [P, N]) for i in range(2)]
        w_hi = sb("w_hi", [P, GROUPS, N], F32R)
        w_lo = sb("w_lo", [P, GROUPS, N], F32R)
        scaled = [sb(f"scaled{i}", [P, N]) for i in range(2)]
        stats2 = [sb(f"stats2{i}", [P, 6]) for i in range(2)]
        mean_var2 = [sb(f"mean_var2{i}", [P, 2]) for i in range(2)]
        var_eps2 = [sb(f"var_eps2{i}", [P, 1]) for i in range(2)]
        rstd2 = [sb(f"rstd2{i}", [P, 1]) for i in range(2)]
        y = [sb(f"y{i}", [P, N]) for i in range(2)]
        yt_hi = [sb(f"yt_hi{i}", [P, N], F32R) for i in range(2)]
        yt_lo = [sb(f"yt_lo{i}", [P, N], F32R) for i in range(2)]
        result = [sb(f"result{i}", [P, N]) for i in range(2)]

        score_bank = [bank(f"score_bank{i}") for i in range(SBANKS)]
        turn_bank = [bank(f"turn_bank{i}") for i in range(2)]
        pv_bank = bank("pv_bank")
        proj_bank = bank("proj_bank")

        params_loaded = sem("params_loaded")
        first_loaded = [[sem(f"first_{a}_loaded{i}") for a in ("x", "ctx")] for i in range(3)]
        tile_loaded = sem("tile_loaded")
        ffn_w_loaded = sem("ffn_w_loaded")
        ctx_now_loaded = sem("ctx_now_loaded")
        stacked = [sem(f"stacked{b}") for b in range(2)]
        stored = [sem(f"stored{i}") for i in range(2)]
        consts_ready = sem("consts_ready")
        ident_zeroed = sem("ident_zeroed")
        ident_ready = sem("ident_ready")
        w_hi_ready = sem("w_hi_ready")
        w_split = sem("w_split")
        gates_ready = sem("gates_ready")
        stats_done = sem("stats_done")
        mean_var_done = sem("mean_var_done")
        var_eps_done = sem("var_eps_done")
        rstd_done = sem("rstd_done")
        xn_done = sem("xn_done")
        ctxn_done = sem("ctxn_done")
        x_hi_done = sem("x_hi_done")
        c_hi_done = sem("c_hi_done")
        x_lo_done = sem("x_lo_done")
        c_lo_done = sem("c_lo_done")
        q_done = sem("q_done")
        k_done = sem("k_done")
        q_hi_done = sem("q_hi_done")
        k_hi_done = sem("k_hi_done")
        q_lo_done = sem("q_lo_done")
        k_lo_done = sem("k_lo_done")
        s_done = sem("s_done")
        s_kept = sem("s_kept")
        s_squared = sem("s_squared")
        scores_done = sem("scores_done")
        max_done = sem("max_done")
        exp_done = sem("exp_done")
        rden_done = sem("rden_done")
        probs_done = sem("probs_done")
        turned = sem("turned")
        turned_kept = sem("turned_kept")
        pv_done = sem("pv_done")
        sums_kept = sem("sums_kept")
        mean_squared = sem("mean_squared")
        var_done = sem("var_done")
        xm_done = sem("xm_done")
        relu_done = sem("relu_done")
        w_scaled = sem("w_scaled")
        w_deq_done = sem("w_deq_done")
        ffn_hi_done = sem("ffn_hi_done")
        ffn_lo_done = sem("ffn_lo_done")
        root_done = sem("root_done")
        scaled_done = sem("scaled_done")
        x2_done = sem("x2_done")
        stats2_done = sem("stats2_done")
        mean_var2_done = sem("mean_var2_done")
        var_eps2_done = sem("var_eps2_done")
        rstd2_done = sem("rstd2_done")
        y_done = sem("y_done")
        y_turned = sem("y_turned")
        yt_hi_done = sem("yt_hi_done")
        yt_lo_done = sem("yt_lo_done")
        ffn_done = sem("ffn_done")
        result_done = sem("result_done")

        def tile_of(tensor, t):
            if isinstance(t, int):
                return tensor[:, t, :]
            return tensor[:, bass.ds(t, 1), :].rearrange("p a n -> p (a n)")

        def half_of(tensor, t, b):
            if isinstance(t, int):
                return tensor[C * b:C * b + C, t, :]
            return tensor[C * b:C * b + C, bass.ds(t, 1), :].rearrange("p a n -> p (a n)")

        def dram_tile(ap, t):
            if isinstance(t, int):
                return ap[t]
            return ap[bass.ds(t, 1)].rearrange("a p n -> p (a n)")

        def held(eng, count):
            return count if isinstance(count, int) else eng.to_reg(count)

        def bank_of(t, which):
            return pv_bank if which == 1 and is_first(t) else proj_bank

        def sums_bank(t, b):
            return proj_bank if isinstance(t, int) and (t, b) == (TILES - 1, 1) else pv_bank

        def over_tiles(eng, body):
            body(0)
            with eng.Fori(1, TILES - 2) as t:
                body(t)
            body(TILES - 2)
            body(TILES - 1)

        def is_first(t):
            return isinstance(t, int) and t == 0

        def has_next(t):
            return not isinstance(t, int) or t + 1 < TILES

        def has_second_next(t):
            return not isinstance(t, int) or t + 2 < TILES

        block = ctx.enter_context(nc.Block())

        @block.sync
        def _(sp):
            def load(t, x_loaded, ctx_loaded):
                sp.dma_start(tile_of(X, t), dram_tile(x_tiles, t)).then_inc(x_loaded, DMA)
                sp.dma_start(tile_of(CTX, t), dram_tile(context_tiles, t)).then_inc(ctx_loaded, DMA)

            def stack(b, *copies):
                for dst, half, src in copies:
                    sp.dma_start(dst[b][C * half:C * half + C, :].bitcast(F32),
                                 src[C * b:C * b + C, :].bitcast(F32)).then_inc(stacked[b], DMA)

            q_hi_copies, q_lo_copies = [(q_stack, 0, q_hi)], [(q_stack, 1, q_lo)]
            k_hi_copies, k_lo_copies = [(k_same, 0, k_hi), (k_cross, 1, k_hi)], [(k_same, 1, k_lo), (k_cross, 0, k_lo)]
            all_copies = q_hi_copies + q_lo_copies + k_hi_copies + k_lo_copies

            load(0, *first_loaded[0])
            sp.dma_start(params_sb[:, :], params).then_inc(params_loaded, DMA)
            load(1, *first_loaded[1])
            sp.wait_ge(q_hi_done, 1)
            stack(0, *q_hi_copies)
            sp.wait_ge(q_lo_done, 1)
            stack(0, *q_lo_copies)
            sp.wait_ge(k_hi_done, 1)
            stack(0, *k_hi_copies)
            sp.wait_ge(k_lo_done, 1)
            stack(0, *k_lo_copies)
            stack(1, *all_copies)
            load(2, *first_loaded[2])
            sp.dma_start(ctx_now[:, :], dram_tile(context_tiles, 0)).then_inc(ctx_now_loaded, DMA)
            def body(t):
                if not has_next(t):
                    return
                sp.wait_ge(q_lo_done, t + 2)
                sp.wait_ge(scores_done, CHUNKS * t + JC)
                stack(0, *q_hi_copies, *q_lo_copies)
                sp.wait_ge(k_hi_done, t + 2)
                stack(0, *k_hi_copies)
                sp.wait_ge(k_lo_done, t + 2)
                stack(0, *k_lo_copies)
                sp.wait_ge(s_done, t + 1)
                sp.dma_start(ctx_now[:, :], dram_tile(context_tiles, t + 1)).then_inc(ctx_now_loaded, DMA)
                sp.wait_ge(scores_done, CHUNKS * t + CHUNKS)
                stack(1, *all_copies)

            body(0)
            load(3, tile_loaded, tile_loaded)
            sp.dma_start(w_int[:, :, :], weight_q_t.rearrange("(g p) o -> p g o", p=P)).then_inc(ffn_w_loaded, DMA)
            for g in range(GROUPS):
                sp.dma_start(sz[:, g, :, :], scales_zeros[g].partition_broadcast(P)).then_inc(ffn_w_loaded, DMA)
            with sp.Fori(1, TILES - 4) as t:
                body(t)
                sp.wait_ge(tile_loaded, 2 * DMA * t)
                load(t + 3, tile_loaded, tile_loaded)
            for t in range(TILES - 4, TILES):
                body(t)
                if t + 3 < TILES:
                    sp.wait_ge(tile_loaded, 2 * DMA * t)
                    load(t + 3, tile_loaded, tile_loaded)

            sp.wait_ge(result_done, 1)
            sp.dma_start(dram_tile(out_tiles, 0), result[0][:, :]).then_inc(stored[0], DMA)
            sp.wait_ge(result_done, 2)
            sp.dma_start(dram_tile(out_tiles, 1), result[1][:, :]).then_inc(stored[1], DMA)
            with sp.Fori(2, TILES - 1, 2) as u:
                for i in range(2):
                    sp.wait_ge(result_done, u + i + 1)
                    sp.dma_start(dram_tile(out_tiles, u + i), result[i][:, :]).then_inc(stored[i], DMA)
            for i in range(2):
                sp.wait_ge(stored[i], DMA * TILES // 2)

        @block.tensor
        def _(pe):
            def project(t, which):
                hi, lo, hi_done, lo_done, done = (
                    (x_hi, x_lo, x_hi_done, x_lo_done, q_done), (c_hi, c_lo, c_hi_done, c_lo_done, k_done))[which]
                into = bank_of(t, which)
                pe.wait_ge(hi_done, t + 1)
                pe.wait_ge(lo_done, t + 1)
                pe.matmul(into[:, :], w_qk_hi[:, which, :], hi[:, :], start=True, stop=False)
                pe.matmul(into[:, :], w_qk_hi[:, which, :], lo[:, :], start=False, stop=False)
                pe.matmul(into[:, :], w_qk_lo[:, which, :], hi[:, :], start=False, stop=True).then_inc(done, 1)

            def scores(t, c):
                b, j = c // JC, c % JC
                if j == 0:
                    pe.wait_ge(stacked[b], STACK * (t + 1))
                if not (is_first(t) and c < SBANKS):
                    pe.wait_ge(exp_done, CHUNKS * t + c - SBANKS + 1)
                q_part = q_stack[b][:, P * j:P * j + P]
                pe.matmul(score_bank[c % SBANKS][:, :], q_part, k_same[b][:, :], start=True, stop=False)
                pe.matmul(score_bank[c % SBANKS][:, :], q_part, k_cross[b][:, :],
                          start=False, stop=True).then_inc(scores_done, 1)

            def turn(t, c):
                pe.wait_ge(probs_done, CHUNKS * t + c + 1)
                if not (is_first(t) and c < 2):
                    pe.wait_ge(turned_kept, CHUNKS * t + c - 1)
                for i in range(JC):
                    last = pe.transpose(turn_bank[c % 2][:, P * i:P * i + P],
                                        probs[c % SBANKS][:, P * i:P * i + P], ident[:, :])
                last.then_inc(turned, 1)

            def weigh(t, b, i):
                if i == 0:
                    pe.wait_ge(turned_kept, CHUNKS * t + JC * b + JC)
                    pe.wait_ge(s_squared, 2 * t + b + 1)
                    if sums_bank(t, b) is proj_bank:
                        pe.wait_ge(s_kept, 2 * t + 2)
                    elif not (is_first(t) and b == 0):
                        pe.wait_ge(sums_kept, 2 * (2 * t + b))
                mm = pe.matmul(sums_bank(t, b)[:, :], values[:, i, b, :, :].rearrange("p a c -> p (a c)"),
                               probs_t[b][:, i, :], start=(i == 0), stop=(i == JC - 1))
                if i == JC - 1:
                    mm.then_inc(pv_done, 1)

            def value_product(t):
                pe.wait_ge(ctx_now_loaded, DMA * (t + 1))
                k_tile = t + 1 if has_next(t) else t
                pe.wait_ge(k_hi_done, k_tile + 1)
                pe.wait_ge(k_lo_done, k_tile + 1)
                for i in range(JC):
                    last = pe.matmul(proj_bank[:, P * i:P * i + P], ctx_now[:, P * i:P * i + P], w_s,
                                     start=True, stop=True)
                last.then_inc(s_done, 1)

            pe.wait_ge(w_split, 1)
            project(0, 0)
            project(0, 1)
            for c in range(AHEAD_S):
                scores(0, c)
            pe.wait_ge(q_lo_done, 1)
            project(1, 0)
            pe.wait_ge(ident_ready, 1)

            def body(t):
                for c in range(CHUNKS):
                    if c + AHEAD_S < CHUNKS:
                        scores(t, c + AHEAD_S)
                    elif has_next(t):
                        scores(t + 1, c + AHEAD_S - CHUNKS)
                    if c == 7 and has_second_next(t):
                        pe.wait_ge(s_kept, 2 * t + 2)
                        project(t + 2, 0)
                    if c == 3 and not is_first(t):
                        weigh(t - 1, 1, 3)
                    if c == 7:
                        weigh(t, 0, 3)
                    turn(t, c)
                    if c == 0 and has_next(t):
                        pe.wait_ge(q_hi_done, t + 2)
                        pe.wait_ge(q_lo_done, t + 2)
                        project(t + 1, 1)
                    if c in (1, 2) and not is_first(t):
                        for i in ((0, 1), (2,))[c - 1]:
                            weigh(t - 1, 1, i)
                    if c in (5, 6):
                        for i in ((0, 1), (2,))[c - 5]:
                            weigh(t, 0, i)
                    if c == 2:
                        value_product(t)

            over_tiles(pe, body)
            for i in range(JC):
                weigh(TILES - 1, 1, i)

            def turn_y(u, i):
                pe.wait_ge(y_done, u + 1)
                if not (isinstance(u, int) and u < 2):
                    pe.wait_ge(yt_lo_done, u - 1)
                for g in range(GROUPS):
                    last = pe.transpose(score_bank[i][:, P * g:P * g + P], y[i][:, P * g:P * g + P], ident[:, :])
                last.then_inc(y_turned, 1)

            def feed_forward(u, i):
                pe.wait_ge(yt_hi_done, u + 1)
                pe.wait_ge(yt_lo_done, u + 1)
                if not (isinstance(u, int) and u < 2):
                    pe.wait_ge(result_done, u - 1)
                for g in range(GROUPS):
                    hi, lo = (a[i][:, P * g:P * g + P] for a in (yt_hi, yt_lo))
                    pe.matmul(score_bank[2 + i][:, :], hi, w_hi[:, g, :], start=(g == 0), stop=False)
                    pe.matmul(score_bank[2 + i][:, :], hi, w_lo[:, g, :], start=False, stop=False)
                    mm = pe.matmul(score_bank[2 + i][:, :], lo, w_hi[:, g, :], start=False,
                                   stop=(g == GROUPS - 1))
                mm.then_inc(ffn_done, 1)

            pe.wait_ge(exp_done, LAST)
            turn_y(0, 0)
            turn_y(1, 1)
            pe.wait_ge(ffn_hi_done, GROUPS)
            pe.wait_ge(ffn_lo_done, GROUPS)
            feed_forward(0, 0)

            def pair(u):
                turn_y(u, 0)
                feed_forward(u - 1, 1)
                turn_y(u + 1, 1)
                feed_forward(u, 0)

            pair(2)
            with pe.Fori(4, TILES - 1, 2) as u:
                pair(u)
            feed_forward(TILES - 1, 1)

        @block.scalar
        def _(act):
            def keep_hi(t, which):
                if which == 0:
                    act.wait_ge(q_done, t + 1)
                    if not is_first(t):
                        act.wait_ge(stacked[0], STACK * t)
                        act.wait_ge(stacked[1], STACK * t)
                    act.activation(q_hi[:, :], proj_bank[:, :], ACT.Identity,
                                   bias=b_qk[:, 0:1]).then_inc(q_hi_done, 1)
                else:
                    act.wait_ge(k_done, t + 1)
                    act.activation(k_hi[:, :], bank_of(t, 1)[:, :], ACT.Identity,
                                   bias=b_qk[:, 1:2]).then_inc(k_hi_done, 1)

            def exponentials(t, c):
                act.wait_ge(max_done, CHUNKS * t + c + 1)
                if not (is_first(t) and c < SBANKS):
                    act.wait_ge(turned, CHUNKS * t + c - SBANKS + 1)
                act.activation(probs[c % SBANKS][:, :], score_bank[c % SBANKS][:, :], ACT.Exp,
                               bias=neg_max[:, c:c + 1], accum_out=den[:, c:c + 1]).then_inc(exp_done, 1)

            def keep_turned(t, c):
                b, j = c // JC, c % JC
                act.wait_ge(turned, CHUNKS * t + c + 1)
                if j == 0 and not is_first(t):
                    act.wait_ge(pv_done, 2 * t + b - 1)
                act.copy(probs_t[b][:, :, P * j:P * j + P],
                         turn_bank[c % 2][:, :].rearrange("p (i n) -> p i n", i=JC)).then_inc(turned_kept, 1)

            def keep_sums(t, b):
                count = held(act, 2 * t + b + 1)
                act.wait_ge(params_loaded, DMA)
                act.wait_ge(pv_done, count)
                act.copy(half_of(MEAN, t, b), sums_bank(t, b)[0:C, :]).then_inc(sums_kept, 1)
                act.copy(half_of(VAR, t, b), sums_bank(t, b)[C:P, :]).then_inc(sums_kept, 1)

            def root(u):
                act.wait_ge(relu_done, u + 1)
                act.activation(tile_of(VAR, u), tile_of(VAR, u), ACT.Sqrt).then_inc(root_done, 1)

            act.wait_ge(params_loaded, DMA)
            act.activation(tanh_g[:, :], gates, ACT.Tanh).then_inc(gates_ready, 1)
            keep_hi(0, 0)
            keep_hi(0, 1)
            for c in range(AHEAD_E):
                exponentials(0, c)
            keep_hi(1, 0)

            def body(t):
                for c in range(CHUNKS):
                    if c == 1 and has_next(t):
                        keep_hi(t + 1, 1)
                    if c + AHEAD_E < CHUNKS:
                        exponentials(t, c + AHEAD_E)
                    elif has_next(t):
                        exponentials(t + 1, c + AHEAD_E - CHUNKS)
                    if c == 0 and not is_first(t):
                        keep_sums(t - 1, 0)
                    if c == 4 and not is_first(t):
                        keep_sums(t - 1, 1)
                    if c > 0:
                        keep_turned(t, c - 1)
                    elif not is_first(t):
                        keep_turned(t - 1, CHUNKS - 1)
                    if c == 7 and has_second_next(t):
                        keep_hi(t + 2, 0)
                    if c >= 6 and not has_next(t):
                        root(c - 6)

            over_tiles(act, body)
            keep_turned(TILES - 1, CHUNKS - 1)
            keep_sums(TILES - 1, 0)
            keep_sums(TILES - 1, 1)

            def keep_y_hi(u, i):
                act.wait_ge(y_turned, u + 1)
                if not (isinstance(u, int) and u < 2):
                    act.wait_ge(ffn_done, u - 1)
                act.copy(yt_hi[i][:, :], score_bank[i][:, :]).then_inc(yt_hi_done, 1)


            def pair(u):
                root(u)
                keep_y_hi(u - 2, 0)
                root(u + 1)
                keep_y_hi(u - 1, 1)

            pair(2)
            with act.Fori(4, TILES - 1, 2) as u:
                pair(u)
            keep_y_hi(TILES - 2, 0)
            keep_y_hi(TILES - 1, 1)

        @block.vector
        def _(dve):
            def statistics(t):
                if isinstance(t, int) and t < 3:
                    dve.wait_ge(first_loaded[t][0], DMA)
                    dve.bn_stats(stats[:, 0, :], tile_of(X, t))
                    dve.wait_ge(first_loaded[t][1], DMA)
                else:
                    count = held(dve, 2 * DMA * (t - 2))
                    dve.wait_ge(params_loaded, DMA)
                    dve.wait_ge(tile_loaded, count)
                    dve.bn_stats(stats[:, 0, :], tile_of(X, t))
                dve.bn_stats(stats[:, 1, :], tile_of(CTX, t)).then_inc(stats_done, 1)
                count = held(dve, t + 1)
                dve.wait_ge(params_loaded, DMA)
                dve.wait_ge(stats_done, count)
                dve.bn_aggr(mean_var[:, 0, :], stats[:, 0, :])
                dve.bn_aggr(mean_var[:, 1, :], stats[:, 1, :]).then_inc(mean_var_done, 1)
                dve.wait_ge(mean_var_done, t + 1)
                dve.tensor_scalar(var_eps[:, 0:1], mean_var[:, 0, 1:2], 1.0 + EPS, EPS * EPS, ALU.mult, ALU.add)
                dve.tensor_scalar(var_eps[:, 1:2], mean_var[:, 1, 1:2], EPS, None,
                                  ALU.add).then_inc(var_eps_done, 1)

            def normalise(t, which):
                dve.wait_ge(rstd_done, t + 1)
                if which == 0:
                    if not is_first(t):
                        dve.wait_ge(x_lo_done, t)
                        dve.wait_ge(q_done, t)
                    dve.tensor_scalar(xn[:, :], tile_of(X, t), mean_var[:, 0, 0:1], rstd[:, 0:1],
                                      ALU.subtract, ALU.mult).then_inc(xn_done, 1)
                    dve.wait_ge(xn_done, t + 1)
                    dve.tensor_copy(x_hi[:, :], xn[:, :]).then_inc(x_hi_done, 1)
                else:
                    if not is_first(t):
                        dve.wait_ge(k_done, t)
                    dve.tensor_scalar(tile_of(CTX, t), tile_of(CTX, t), mean_var[:, 1, 0:1], rstd[:, 1:2],
                                      ALU.subtract, ALU.mult).then_inc(ctxn_done, 1)
                    count = held(dve, t + 1)
                    dve.wait_ge(params_loaded, DMA)
                    dve.wait_ge(ctxn_done, count)
                    dve.tensor_copy(c_hi[:, :], tile_of(CTX, t)).then_inc(c_hi_done, 1)

            def keep_lo(t, which):
                hi, lo, hi_done, lo_done = ((q_hi, q_lo, q_hi_done, q_lo_done),
                                            (k_hi, k_lo, k_hi_done, k_lo_done))[which]
                dve.wait_ge(hi_done, t + 1)
                dve.scalar_tensor_tensor(lo[:, :], bank_of(t, which)[:, :], b_qk[:, which:which + 1],
                                         hi[:, :].bitcast(F32), ALU.add, ALU.subtract).then_inc(lo_done, 1)

            def maximum(t, c):
                dve.wait_ge(scores_done, CHUNKS * t + c + 1)
                dve.tensor_reduce(neg_max[:, c:c + 1], score_bank[c % SBANKS][:, :], AX_X, ALU.max,
                                  negate=True).then_inc(max_done, 1)

            def reciprocal(t, c):
                dve.wait_ge(exp_done, CHUNKS * t + c + 1)
                dve.reciprocal(rden[:, c:c + 1], den[:, c:c + 1]).then_inc(rden_done, 1)

            def with_mean(t):
                dve.wait_ge(sums_kept, 4 * (t + 1))
                dve.scalar_tensor_tensor(tile_of(X, t), tile_of(MEAN, t), tanh_g[:, 0:1], tile_of(X, t),
                                         ALU.mult, ALU.add).then_inc(xm_done, 1)

            def square_mean(t):
                if not is_first(t):
                    dve.wait_ge(var_done, t)
                dve.tensor_tensor(mean_sq[:, :], tile_of(MEAN, t), tile_of(MEAN, t),
                                  ALU.mult).then_inc(mean_squared, 1)

            def variance(t):
                dve.wait_ge(mean_squared, t + 1)
                dve.tensor_tensor(tile_of(VAR, t), tile_of(VAR, t), mean_sq[:, :],
                                  ALU.subtract).then_inc(var_done, 1)

            def relu(t):
                dve.wait_ge(var_done, t + 1)
                dve.tensor_scalar(tile_of(VAR, t), tile_of(VAR, t), 0.0, None, ALU.max).then_inc(relu_done, 1)

            def keep_values(t, b):
                dve.wait_ge(s_done, t + 1)
                if b == 1 and not is_first(t):
                    dve.wait_ge(pv_done, 2 * t)
                dve.tensor_tensor(values[:, :, b, 0, :],
                                  proj_bank[:, :].rearrange("p (i b c) -> p i b c", b=2, c=C)[:, :, b, :],
                                  b_s.unsqueeze(1).broadcast_to([P, JC, C]),
                                  ALU.add).then_inc(s_kept, 1)

            def after_attention(u, i):
                dve.wait_ge(scaled_done, u + 1)
                dve.scalar_tensor_tensor(tile_of(X, u), scaled[i][:, :], tanh_g[:, 0:1], tile_of(X, u),
                                         ALU.mult, ALU.add).then_inc(x2_done, 1)
                count = held(dve, u + 1)
                dve.wait_ge(params_loaded, DMA)
                dve.wait_ge(x2_done, count)
                dve.bn_stats(stats2[i][:, :], tile_of(X, u)).then_inc(stats2_done, 1)
                count = held(dve, u + 1)
                dve.wait_ge(params_loaded, DMA)
                dve.wait_ge(stats2_done, count)
                dve.bn_aggr(mean_var2[i][:, :], stats2[i][:, :]).then_inc(mean_var2_done, 1)
                dve.wait_ge(mean_var2_done, u + 1)
                dve.tensor_scalar(var_eps2[i][:, :], mean_var2[i][:, 1:2], EPS, None,
                                  ALU.add).then_inc(var_eps2_done, 1)

            def normalise_y(u, i):
                dve.wait_ge(rstd2_done, u + 1)
                if not (isinstance(u, int) and u < 2):
                    dve.wait_ge(y_turned, u - 1)
                dve.tensor_scalar(y[i][:, :], tile_of(X, u), mean_var2[i][:, 0:1], rstd2[i][:, :],
                                  ALU.subtract, ALU.mult).then_inc(y_done, 1)

            def scale_weights(g):
                if g >= 2:
                    dve.wait_ge(ffn_lo_done, g - 1)
                else:
                    dve.wait_ge(ffn_w_loaded, (1 + GROUPS) * DMA)
                dve.scalar_tensor_tensor(w_deq[g % 2][:, :], w_int[:, g, :], -QUANT_ZERO, sz[:, g, 0, :],
                                         ALU.add, ALU.mult).then_inc(w_scaled, 1)

            def weights_hi(g):
                dve.wait_ge(w_deq_done, g + 1)
                dve.tensor_copy(w_hi[:, g, :], w_deq[g % 2][:, :]).then_inc(ffn_hi_done, 1)

            statistics(0)
            dve.wait_ge(params_loaded, DMA)
            dve.tensor_copy(w_qk_hi[:, :, :], w_qk).then_inc(w_hi_ready, 1)
            dve.wait_ge(w_hi_ready, 1)
            dve.tensor_tensor(w_qk_lo[:, :, :], w_qk, w_qk_hi[:, :, :].bitcast(F32),
                              ALU.subtract).then_inc(w_split, 1)
            normalise(0, 0)
            normalise(0, 1)
            keep_lo(0, 0)
            keep_lo(0, 1)
            statistics(1)
            normalise(1, 0)
            normalise(1, 1)
            dve.wait_ge(gates_ready, 1)
            for c in range(AHEAD_S):
                maximum(0, c)
                if c > 0:
                    reciprocal(0, c - 1)
            keep_lo(1, 0)

            def body(t):
                for c in range(CHUNKS):
                    if c + AHEAD_S < CHUNKS:
                        maximum(t, c + AHEAD_S)
                    elif has_next(t):
                        maximum(t + 1, c + AHEAD_S - CHUNKS)
                    if c + AHEAD_E < CHUNKS:
                        reciprocal(t, c + AHEAD_E)
                    elif has_next(t):
                        reciprocal(t + 1, c + AHEAD_E - CHUNKS)
                    if c == 1 and has_next(t):
                        keep_lo(t + 1, 1)
                    if not is_first(t):
                        if c == 5:
                            with_mean(t - 1)
                            square_mean(t - 1)
                        if c == 6:
                            variance(t - 1)
                        if c == 7:
                            relu(t - 1)
                    if c == 3:
                        keep_values(t, 0)
                    if c == 4:
                        keep_values(t, 1)
                    if has_second_next(t):
                        if c == 2:
                            statistics(t + 2)
                        if c == 4:
                            normalise(t + 2, 0)
                        if c == 6:
                            normalise(t + 2, 1)
                        if c == 7:
                            keep_lo(t + 2, 0)
                    else:
                        g = (t - TILES + 2) * (GROUPS // 2)
                        late = 3 * (t - TILES + 2)
                        if c == 0:
                            scale_weights(g)
                        if c == 1:
                            weights_hi(g)
                        if c == 5 - late:
                            scale_weights(g + 1)
                        if c == 6 - late:
                            weights_hi(g + 1)

            over_tiles(dve, body)
            after_attention(0, 0)
            after_attention(1, 1)
            normalise_y(0, 0)
            normalise_y(1, 1)
            with_mean(TILES - 1)
            square_mean(TILES - 1)
            variance(TILES - 1)
            relu(TILES - 1)

            def keep_y_lo(u, i):
                dve.wait_ge(yt_hi_done, u + 1)
                dve.tensor_tensor(yt_lo[i][:, :], score_bank[i][:, :], yt_hi[i][:, :].bitcast(F32),
                                  ALU.subtract).then_inc(yt_lo_done, 1)

            def add_ffn(u, i):
                dve.wait_ge(ffn_done, u + 1)
                if not (isinstance(u, int) and u < 2):
                    dve.wait_ge(stored[i], DMA // 2 * (u - i))
                dve.scalar_tensor_tensor(result[i][:, :], score_bank[2 + i][:, :], tanh_g[:, 1:2],
                                         tile_of(X, u), ALU.mult, ALU.add).then_inc(result_done, 1)

            def step(u, i):
                keep_y_lo(u, i)
                if u + 2 < TILES:
                    after_attention(u + 2, i)
                if u > 0:
                    add_ffn(u - 1, 1 - i)
                if u + 2 < TILES:
                    normalise_y(u + 2, i)

            for u in range(TILES):
                step(u, u % 2)
            add_ffn(TILES - 1, 1)

        @block.gpsimd
        def _(pool):
            def inverse_deviation(t):
                pool.wait_ge(var_eps_done, t + 1)
                pool.tensor_tensor(rstd[:, :], var_eps[:, :], power[:, :], ALU.pow).then_inc(rstd_done, 1)

            def split_lo(t, which):
                whole, hi, lo, hi_done, lo_done, used = (
                    (xn[:, :], x_hi, x_lo, x_hi_done, x_lo_done, q_done),
                    (tile_of(CTX, t), c_hi, c_lo, c_hi_done, c_lo_done, k_done))[which]
                pool.wait_ge(hi_done, t + 1)
                if not is_first(t):
                    pool.wait_ge(used, t)
                pool.tensor_tensor(lo[:, :], whole, hi[:, :].bitcast(F32), ALU.subtract).then_inc(lo_done, 1)

            def normalise_probs(t, c):
                count = held(pool, CHUNKS * t + c + 1)
                pool.wait_ge(ident_ready, 1)
                pool.wait_ge(rden_done, count)
                pool.tensor_scalar(probs[c % SBANKS][:, :], probs[c % SBANKS][:, :], rden[:, c:c + 1], 1.0,
                                   ALU.mult, ALU.mult).then_inc(probs_done, 1)

            def square_values(t, b):
                pool.wait_ge(s_kept, 2 * t + b + 1)
                pool.tensor_tensor(values[:, :, b, 1, :], values[:, :, b, 0, :], values[:, :, b, 0, :],
                                   ALU.mult).then_inc(s_squared, 1)

            def dequantise(g):
                pool.wait_ge(w_scaled, g + 1)
                pool.tensor_tensor(w_deq[g % 2][:, :], w_deq[g % 2][:, :], sz[:, g, 1, :],
                                   ALU.add).then_inc(w_deq_done, 1)

            def weights_lo(g):
                pool.wait_ge(ffn_hi_done, g + 1)
                pool.tensor_tensor(w_lo[:, g, :], w_deq[g % 2][:, :], w_hi[:, g, :].bitcast(F32),
                                   ALU.subtract).then_inc(ffn_lo_done, 1)

            pool.memset(ident[:, :], 0.0).then_inc(ident_zeroed, 1)
            pool.memset(power[:, :], -0.5).then_inc(consts_ready, 1)
            pool.wait_ge(ident_zeroed, 1)
            pool.affine_select(out=ident[:, :], in_=ident[:, :], compare_op=ALU.not_equal, fill=1.0, base=0,
                               pattern=[[-1, P]], channel_multiplier=1).then_inc(ident_ready, 1)
            pool.wait_ge(consts_ready, 1)
            inverse_deviation(0)
            split_lo(0, 0)
            split_lo(0, 1)
            inverse_deviation(1)
            split_lo(1, 0)
            split_lo(1, 1)
            for c in range(AHEAD_E):
                normalise_probs(0, c)

            def body(t):
                for c in range(CHUNKS):
                    if c + AHEAD_E < CHUNKS:
                        normalise_probs(t, c + AHEAD_E)
                    elif has_next(t):
                        normalise_probs(t + 1, c + AHEAD_E - CHUNKS)
                    if c == 3:
                        square_values(t, 0)
                    if c == 4:
                        square_values(t, 1)
                    if has_second_next(t):
                        if c == 2:
                            inverse_deviation(t + 2)
                        if c == 5:
                            split_lo(t + 2, 0)
                        if c == 6:
                            split_lo(t + 2, 1)
                    else:
                        g = (t - TILES + 2) * (GROUPS // 2)
                        late = 3 * (t - TILES + 2)
                        if c == 0:
                            dequantise(g)
                        if c == 1:
                            weights_lo(g)
                        if c == 5 - late:
                            dequantise(g + 1)
                        if c == 6 - late:
                            weights_lo(g + 1)

            over_tiles(pool, body)

            def scale_context(u, i):
                pool.wait_ge(root_done, u + 1)
                if not (isinstance(u, int) and u < 2):
                    pool.wait_ge(x2_done, u - 1)
                pool.tensor_tensor(scaled[i][:, :], tile_of(CTX, u), tile_of(VAR, u),
                                   ALU.mult).then_inc(scaled_done, 1)

            def inverse_deviation2(u, i):
                pool.wait_ge(var_eps2_done, u + 1)
                if not (isinstance(u, int) and u < 2):
                    pool.wait_ge(y_done, u - 1)
                pool.tensor_tensor(rstd2[i][:, :], var_eps2[i][:, :], power[:, 0:1],
                                   ALU.pow).then_inc(rstd2_done, 1)

            scale_context(0, 0)
            scale_context(1, 1)
            inverse_deviation2(0, 0)
            inverse_deviation2(1, 1)
            with pool.Fori(2, TILES - 1, 2) as u:
                for i in range(2):
                    scale_context(u + i, i)
                for i in range(2):
                    inverse_deviation2(u + i, i)


def kernel(**inputs):
    import numpy as np
    import concourse.bacc as bacc
    from concourse.bass_utils import run_bass_kernel_spmd as run

    def laid(name, order=None):
        a = np.asarray(inputs[name])
        return np.ascontiguousarray(a if order is None else a.transpose(order))

    C = inputs["L0_xattn_Wq"].shape[0]
    params = np.zeros((P, 3 * P + 4 + C), np.float32)
    for half in range(2):
        rows = slice(C * half, C * half + C)
        for n, name in enumerate(("L0_xattn_Wq", "L0_xattn_Wk", "L0_xattn_Ws")):
            params[rows, P * n + C * half:P * n + C * half + C] = laid(name, (1, 0))
        for n, name in enumerate(("L0_xattn_bq", "L0_xattn_bk")):
            params[rows, 3 * P + n] = laid(name)
    for n, name in enumerate(("g_xattn", "g_ffn")):
        params[:, 3 * P + 2 + n] = laid(name)
    params[:, 3 * P + 4:] = laid("L0_xattn_bs_")
    arrays = {
        "x": laid("x"),
        "context": laid("ctx_4096"),
        "params": params,
        "weight_q_t": laid("L0_ffn_weight_q", (1, 0)),
        "scales_zeros": laid("L0_ffn_scales_and_zeros", (0, 2, 1)),
    }
    nc = bacc.Bacc("TRN2", target_bir_lowering=False, num_devices=1)
    args = [nc.dram_tensor(f"in_{n}", a.shape, mybir.dt.from_np(a.dtype), kind="ExternalInput").ap()
            for n, a in arrays.items()]
    out = nc.dram_tensor("out_0", arrays["x"].shape, F32, kind="ExternalOutput").ap()
    gated_attention_ffn(nc, *args, out)
    r = run(nc, [{f"in_{n}": a for n, a in arrays.items()}], core_ids=[0])
    return r.results[0]["out_0"]
```

```python
from contextlib import ExitStack

import concourse.bass as bass
from concourse import mybir

F32 = mybir.dt.float32
F32R = mybir.dt.float32r
I32 = mybir.dt.int32
ALU = mybir.AluOpType
ACT = mybir.ActivationFunctionType
AX_X = mybir.AxisListType.X

EPS = 1e-5
QUANT_ZERO = 8.0
P = 128


def gated_attention_ffn(nc, x, context, params, weight_q_t, scales_zeros, out):
    BATCHES, C, N = x.shape
    TILES = BATCHES // 2
    JC = N // P
    CHUNKS = 2 * JC
    GROUPS = weight_q_t.shape[0] // P
    AHEAD_S, AHEAD_E = 3, 2
    SBANKS = 4
    LAST = CHUNKS * TILES
    DMA = 16
    STACK = 6 * DMA
    assert 2 * C == P and N == 512 and CHUNKS % SBANKS == 0

    x_tiles = x.rearrange("(t b) c n -> t (b c) n", b=2)
    context_tiles = context.rearrange("(t b) c n -> t (b c) n", b=2)
    out_tiles = out.rearrange("(t b) c n -> t (b c) n", b=2)

    with ExitStack() as ctx:
        def sb(name, shape, dt=F32):
            return ctx.enter_context(nc.sbuf_tensor(name, shape, dt))

        def bank(name):
            return ctx.enter_context(nc.psum_tensor(name, [P, 512], F32))

        def sem(name):
            return ctx.enter_context(nc.semaphore(name))

        X = sb("X", [P, TILES, N])
        CTX = sb("CTX", [P, TILES, N])
        MEAN = sb("MEAN", [P, TILES, N])
        VAR = sb("VAR", [P, TILES, N])
        params_sb = sb("params_sb", [P, params.shape[1]])
        w_qk = params_sb[:, 0:2 * P].rearrange("p (w o) -> p w o", w=2)
        w_s = params_sb[:, 2 * P:3 * P]
        b_qk = params_sb[:, 3 * P:3 * P + 2]
        gates = params_sb[:, 3 * P + 2:3 * P + 4]
        b_s = params_sb[:, 3 * P + 4:3 * P + 4 + C]
        w_qk_hi = sb("w_qk_hi", [P, 2, P], F32R)
        w_qk_lo = sb("w_qk_lo", [P, 2, P], F32R)
        xn = sb("xn", [P, N])
        x_hi = sb("x_hi", [P, N], F32R)
        x_lo = sb("x_lo", [P, N], F32R)
        c_hi = sb("c_hi", [P, N], F32R)
        c_lo = sb("c_lo", [P, N], F32R)
        ctx_now = sb("ctx_now", [P, N])
        stats = sb("stats", [P, 2, 6])
        mean_var = sb("mean_var", [P, 2, 2])
        var_eps = sb("var_eps", [P, 2])
        rstd = sb("rstd", [P, 2])
        q_hi = sb("q_hi", [P, N], F32R)
        q_lo = sb("q_lo", [P, N], F32R)
        k_hi = sb("k_hi", [P, N], F32R)
        k_lo = sb("k_lo", [P, N], F32R)
        q_stack = [sb(f"q_stack{b}", [P, N], F32R) for b in range(2)]
        k_same = [sb(f"k_same{b}", [P, N], F32R) for b in range(2)]
        k_cross = [sb(f"k_cross{b}", [P, N], F32R) for b in range(2)]
        probs = [sb(f"probs{i}", [P, N]) for i in range(SBANKS)]
        neg_max = sb("neg_max", [P, CHUNKS])
        den = sb("den", [P, CHUNKS])
        rden = sb("rden", [P, CHUNKS])
        probs_t = [sb(f"probs_t{b}", [P, JC, N]) for b in range(2)]
        values = sb("values", [P, JC, 2, 2, C])
        mean_sq = sb("mean_sq", [P, N])
        ident = sb("ident", [P, P])
        power = sb("power", [P, 2])
        tanh_g = sb("tanh_g", [P, 2])
        w_int = sb("w_int", [P, GROUPS, N], I32)
        sz = sb("sz", [P, GROUPS, 2, N])
        w_deq = [sb(f"w_deq{i}", [P, N]) for i in range(2)]
        w_hi = sb("w_hi", [P, GROUPS, N], F32R)
        w_lo = sb("w_lo", [P, GROUPS, N], F32R)
        stats2 = sb("stats2", [P, TILES, 6])
        mean_var2 = sb("mean_var2", [P, TILES, 2])
        neg_mean2 = sb("neg_mean2", [P, TILES])
        var_eps2 = sb("var_eps2", [P, TILES])
        rstd2 = sb("rstd2", [P, TILES])
        shift2 = sb("shift2", [P, TILES])
        y = [sb(f"y{i}", [P, N]) for i in range(2)]
        yt_hi = [sb(f"yt_hi{i}", [P, N], F32R) for i in range(2)]
        yt_lo = [sb(f"yt_lo{i}", [P, N], F32R) for i in range(2)]
        result = [sb(f"result{i}", [P, N]) for i in range(2)]

        score_bank = [bank(f"score_bank{i}") for i in range(SBANKS)]
        turn_bank = [bank(f"turn_bank{i}") for i in range(2)]
        pv_bank = bank("pv_bank")
        proj_bank = bank("proj_bank")

        params_loaded = sem("params_loaded")
        first_loaded = [[sem(f"first_{a}_loaded{i}") for a in ("x", "ctx")] for i in range(3)]
        tile_loaded = sem("tile_loaded")
        ffn_w_loaded = sem("ffn_w_loaded")
        ctx_now_loaded = sem("ctx_now_loaded")
        stacked = [sem(f"stacked{b}") for b in range(2)]
        stored = [sem(f"stored{i}") for i in range(2)]
        consts_ready = sem("consts_ready")
        ident_zeroed = sem("ident_zeroed")
        ident_ready = sem("ident_ready")
        w_hi_ready = sem("w_hi_ready")
        w_split = sem("w_split")
        gates_ready = sem("gates_ready")
        first_x_stats_done = sem("first_x_stats_done")
        first_x_mean_var_done = sem("first_x_mean_var_done")
        first_x_var_eps_done = sem("first_x_var_eps_done")
        first_x_rstd_done = sem("first_x_rstd_done")
        stats_done = sem("stats_done")
        mean_var_done = sem("mean_var_done")
        var_eps_done = sem("var_eps_done")
        rstd_done = sem("rstd_done")
        xn_done = sem("xn_done")
        ctxn_done = sem("ctxn_done")
        x_hi_done = sem("x_hi_done")
        c_hi_done = sem("c_hi_done")
        x_lo_done = sem("x_lo_done")
        c_lo_done = sem("c_lo_done")
        q_done = sem("q_done")
        k_done = sem("k_done")
        q_hi_done = sem("q_hi_done")
        k_hi_done = sem("k_hi_done")
        q_lo_done = sem("q_lo_done")
        k_lo_done = sem("k_lo_done")
        s_done = sem("s_done")
        s_kept = sem("s_kept")
        s_squared = sem("s_squared")
        scores_done = sem("scores_done")
        max_done = sem("max_done")
        exp_done = sem("exp_done")
        rden_done = sem("rden_done")
        probs_done = sem("probs_done")
        turned = sem("turned")
        turned_kept = sem("turned_kept")
        pv_done = sem("pv_done")
        sums_kept = sem("sums_kept")
        mean_squared = sem("mean_squared")
        var_done = sem("var_done")
        relu_done = sem("relu_done")
        w_scaled = sem("w_scaled")
        w_deq_done = sem("w_deq_done")
        ffn_hi_done = sem("ffn_hi_done")
        ffn_lo_done = sem("ffn_lo_done")
        root_done = sem("root_done")
        scaled_done = sem("scaled_done")
        x2_done = sem("x2_done")
        stats2_done = sem("stats2_done")
        mean_var2_done = sem("mean_var2_done")
        var_eps2_done = sem("var_eps2_done")
        rstd2_done = sem("rstd2_done")
        shift2_done = sem("shift2_done")
        y_done = sem("y_done")
        y_turned = sem("y_turned")
        yt_hi_done = sem("yt_hi_done")
        yt_lo_done = sem("yt_lo_done")
        ffn_done = sem("ffn_done")
        result_done = sem("result_done")

        def tile_of(tensor, t):
            if isinstance(t, int):
                return tensor[:, t, :]
            return tensor[:, bass.ds(t, 1), :].rearrange("p a n -> p (a n)")

        def half_of(tensor, t, b):
            if isinstance(t, int):
                return tensor[C * b:C * b + C, t, :]
            return tensor[C * b:C * b + C, bass.ds(t, 1), :].rearrange("p a n -> p (a n)")

        def dram_tile(ap, t):
            if isinstance(t, int):
                return ap[t]
            return ap[bass.ds(t, 1)].rearrange("a p n -> p (a n)")

        def held(eng, count):
            return count if isinstance(count, int) else eng.to_reg(count)

        def bank_of(t, which):
            return pv_bank if which == 1 and is_first(t) else proj_bank

        def sums_bank(t, b):
            return proj_bank if isinstance(t, int) and (t, b) == (TILES - 1, 1) else pv_bank

        def over_tiles(eng, body):
            body(0)
            with eng.Fori(1, TILES - 2) as t:
                body(t)
            body(TILES - 2)
            body(TILES - 1)

        def is_first(t):
            return isinstance(t, int) and t == 0

        def has_next(t):
            return not isinstance(t, int) or t + 1 < TILES

        def has_second_next(t):
            return not isinstance(t, int) or t + 2 < TILES

        block = ctx.enter_context(nc.Block())

        @block.sync
        def _(sp):
            def load(t, x_loaded, ctx_loaded):
                sp.dma_start(tile_of(X, t), dram_tile(x_tiles, t)).then_inc(x_loaded, DMA)
                sp.dma_start(tile_of(CTX, t), dram_tile(context_tiles, t)).then_inc(ctx_loaded, DMA)

            def stack(b, *copies):
                for dst, half, src in copies:
                    sp.dma_start(dst[b][C * half:C * half + C, :].bitcast(F32),
                                 src[C * b:C * b + C, :].bitcast(F32)).then_inc(stacked[b], DMA)

            q_hi_copies, q_lo_copies = [(q_stack, 0, q_hi)], [(q_stack, 1, q_lo)]
            k_hi_copies, k_lo_copies = [(k_same, 0, k_hi), (k_cross, 1, k_hi)], [(k_same, 1, k_lo), (k_cross, 0, k_lo)]
            all_copies = q_hi_copies + q_lo_copies + k_hi_copies + k_lo_copies

            load(0, *first_loaded[0])
            sp.dma_start(params_sb[:, :], params).then_inc(params_loaded, DMA)
            load(1, *first_loaded[1])
            sp.wait_ge(q_hi_done, 1)
            stack(0, *q_hi_copies)
            sp.wait_ge(q_lo_done, 1)
            stack(0, *q_lo_copies)
            sp.wait_ge(k_lo_done, 1)
            stack(1, *all_copies)
            load(2, *first_loaded[2])
            sp.dma_start(ctx_now[:, :], dram_tile(context_tiles, 0)).then_inc(ctx_now_loaded, DMA)

            def body(t):
                if not has_next(t):
                    return
                sp.wait_ge(q_lo_done, t + 2)
                sp.wait_ge(scores_done, CHUNKS * t + JC)
                stack(0, *q_hi_copies, *q_lo_copies)
                sp.wait_ge(k_hi_done, t + 2)
                stack(0, *k_hi_copies)
                sp.wait_ge(k_lo_done, t + 2)
                stack(0, *k_lo_copies)
                sp.wait_ge(s_done, t + 1)
                sp.dma_start(ctx_now[:, :], dram_tile(context_tiles, t + 1)).then_inc(ctx_now_loaded, DMA)
                sp.wait_ge(scores_done, CHUNKS * t + CHUNKS)
                stack(1, *all_copies)

            body(0)
            load(3, tile_loaded, tile_loaded)
            sp.dma_start(w_int[:, :, :], weight_q_t.rearrange("(g p) o -> p g o", p=P)).then_inc(ffn_w_loaded, DMA)
            for g in range(GROUPS):
                sp.dma_start(sz[:, g, :, :], scales_zeros[g].partition_broadcast(P)).then_inc(ffn_w_loaded, DMA)
            with sp.Fori(1, TILES - 4) as t:
                body(t)
                sp.wait_ge(tile_loaded, 2 * DMA * t)
                load(t + 3, tile_loaded, tile_loaded)
            for t in range(TILES - 4, TILES):
                body(t)
                if t + 3 < TILES:
                    sp.wait_ge(tile_loaded, 2 * DMA * t)
                    load(t + 3, tile_loaded, tile_loaded)

            sp.wait_ge(result_done, 1)
            sp.dma_start(dram_tile(out_tiles, 0), result[0][:, :]).then_inc(stored[0], DMA)
            sp.wait_ge(result_done, 2)
            sp.dma_start(dram_tile(out_tiles, 1), result[1][:, :]).then_inc(stored[1], DMA)
            with sp.Fori(2, TILES - 1, 2) as u:
                for i in range(2):
                    sp.wait_ge(result_done, u + i + 1)
                    sp.dma_start(dram_tile(out_tiles, u + i), result[i][:, :]).then_inc(stored[i], DMA)
            for i in range(2):
                sp.wait_ge(stored[i], DMA * TILES // 2)

        @block.tensor
        def _(pe):
            def project(t, which):
                hi, lo, hi_done, lo_done, done = (
                    (x_hi, x_lo, x_hi_done, x_lo_done, q_done), (c_hi, c_lo, c_hi_done, c_lo_done, k_done))[which]
                into = bank_of(t, which)
                pe.wait_ge(hi_done, t + 1)
                pe.wait_ge(lo_done, t + 1)
                pe.matmul(into[:, :], w_qk_hi[:, which, :], hi[:, :], start=True, stop=False)
                pe.matmul(into[:, :], w_qk_hi[:, which, :], lo[:, :], start=False, stop=False)
                pe.matmul(into[:, :], w_qk_lo[:, which, :], hi[:, :], start=False, stop=True).then_inc(done, 1)

            def scores(t, c):
                b, j = c // JC, c % JC
                if j == 0:
                    pe.wait_ge(stacked[b], STACK * (t + 1))
                if not (is_first(t) and c < SBANKS):
                    pe.wait_ge(exp_done, CHUNKS * t + c - SBANKS + 1)
                q_part = q_stack[b][:, P * j:P * j + P]
                pe.matmul(score_bank[c % SBANKS][:, :], q_part, k_same[b][:, :], start=True, stop=False)
                pe.matmul(score_bank[c % SBANKS][:, :], q_part, k_cross[b][:, :],
                          start=False, stop=True).then_inc(scores_done, 1)

            def turn(t, c):
                pe.wait_ge(probs_done, CHUNKS * t + c + 1)
                if not (is_first(t) and c < 2):
                    pe.wait_ge(turned_kept, CHUNKS * t + c - 1)
                for i in range(JC):
                    last = pe.transpose(turn_bank[c % 2][:, P * i:P * i + P],
                                        probs[c % SBANKS][:, P * i:P * i + P], ident[:, :])
                last.then_inc(turned, 1)

            def weigh(t, b, i):
                if i == 0:
                    pe.wait_ge(turned_kept, CHUNKS * t + JC * b + JC)
                    pe.wait_ge(s_squared, 2 * t + b + 1)
                    if sums_bank(t, b) is proj_bank:
                        pe.wait_ge(s_kept, 2 * t + 2)
                    elif not (is_first(t) and b == 0):
                        pe.wait_ge(sums_kept, 2 * (2 * t + b))
                mm = pe.matmul(sums_bank(t, b)[:, :], values[:, i, b, :, :].rearrange("p a c -> p (a c)"),
                               probs_t[b][:, i, :], start=(i == 0), stop=(i == JC - 1))
                if i == JC - 1:
                    mm.then_inc(pv_done, 1)

            def value_product(t):
                pe.wait_ge(ctx_now_loaded, DMA * (t + 1))
                k_tile = t + 1 if has_next(t) else t
                pe.wait_ge(k_hi_done, k_tile + 1)
                pe.wait_ge(k_lo_done, k_tile + 1)
                for i in range(JC):
                    last = pe.matmul(proj_bank[:, P * i:P * i + P], ctx_now[:, P * i:P * i + P], w_s,
                                     start=True, stop=True)
                last.then_inc(s_done, 1)

            pe.wait_ge(w_split, 1)
            project(0, 0)
            project(0, 1)
            for c in range(AHEAD_S):
                scores(0, c)
            pe.wait_ge(q_lo_done, 1)
            project(1, 0)
            pe.wait_ge(ident_ready, 1)

            def body(t):
                for c in range(CHUNKS):
                    if c + AHEAD_S < CHUNKS:
                        scores(t, c + AHEAD_S)
                    elif has_next(t):
                        scores(t + 1, c + AHEAD_S - CHUNKS)
                    if c == 7 and has_second_next(t):
                        pe.wait_ge(s_kept, 2 * t + 2)
                        project(t + 2, 0)
                    if c == 3 and not is_first(t):
                        weigh(t - 1, 1, 3)
                    if c == 7 and has_next(t):
                        weigh(t, 0, 3)
                    turn(t, c)
                    if c == 7 and not has_next(t):
                        weigh(t, 0, 3)
                    if c == (1 if is_first(t) else 0) and has_next(t):
                        pe.wait_ge(q_hi_done, t + 2)
                        pe.wait_ge(q_lo_done, t + 2)
                        project(t + 1, 1)
                    if c in (1, 2) and not is_first(t):
                        for i in ((0, 1), (2,))[c - 1]:
                            weigh(t - 1, 1, i)
                    if c in (5, 6):
                        for i in ((0, 1), (2,))[c - 5]:
                            weigh(t, 0, i)
                    if c == 2:
                        value_product(t)

            over_tiles(pe, body)
            for i in range(JC):
                weigh(TILES - 1, 1, i)

            def turn_y(u, i):
                pe.wait_ge(y_done, u + 1)
                if not (isinstance(u, int) and u < 2):
                    pe.wait_ge(yt_lo_done, u - 1)
                for g in range(GROUPS):
                    last = pe.transpose(score_bank[i][:, P * g:P * g + P], y[i][:, P * g:P * g + P], ident[:, :])
                last.then_inc(y_turned, 1)

            def feed_forward(u, i):
                pe.wait_ge(yt_hi_done, u + 1)
                if not (isinstance(u, int) and u < 2):
                    pe.wait_ge(result_done, u - 1)
                for g in range(GROUPS):
                    hi = yt_hi[i][:, P * g:P * g + P]
                    pe.matmul(score_bank[2 + i][:, :], hi, w_hi[:, g, :], start=(g == 0), stop=False)
                    pe.matmul(score_bank[2 + i][:, :], hi, w_lo[:, g, :], start=False, stop=False)
                pe.wait_ge(yt_lo_done, u + 1)
                for g in range(GROUPS):
                    mm = pe.matmul(score_bank[2 + i][:, :], yt_lo[i][:, P * g:P * g + P], w_hi[:, g, :],
                                   start=False, stop=(g == GROUPS - 1))
                mm.then_inc(ffn_done, 1)

            pe.wait_ge(exp_done, LAST)
            turn_y(0, 0)
            turn_y(1, 1)
            pe.wait_ge(ffn_hi_done, GROUPS)
            pe.wait_ge(ffn_lo_done, GROUPS)
            feed_forward(0, 0)

            def pair(u):
                turn_y(u, 0)
                feed_forward(u - 1, 1)
                turn_y(u + 1, 1)
                feed_forward(u, 0)

            pair(2)
            with pe.Fori(4, TILES - 1, 2) as u:
                pair(u)
            feed_forward(TILES - 1, 1)

        @block.scalar
        def _(act):
            def keep_hi(t, which):
                if which == 0:
                    act.wait_ge(q_done, t + 1)
                    if not is_first(t):
                        act.wait_ge(stacked[0], STACK * t)
                        act.wait_ge(stacked[1], STACK * t)
                    act.activation(q_hi[:, :], proj_bank[:, :], ACT.Identity,
                                   bias=b_qk[:, 0:1]).then_inc(q_hi_done, 1)
                else:
                    act.wait_ge(k_done, t + 1)
                    act.activation(k_hi[:, :], bank_of(t, 1)[:, :], ACT.Identity,
                                   bias=b_qk[:, 1:2]).then_inc(k_hi_done, 1)

            def exponentials(t, c):
                act.wait_ge(max_done, CHUNKS * t + c + 1)
                if not (is_first(t) and c < SBANKS):
                    act.wait_ge(turned, CHUNKS * t + c - SBANKS + 1)
                act.activation(probs[c % SBANKS][:, :], score_bank[c % SBANKS][:, :], ACT.Exp,
                               bias=neg_max[:, c:c + 1], accum_out=den[:, c:c + 1]).then_inc(exp_done, 1)

            def keep_turned(t, c):
                b, j = c // JC, c % JC
                act.wait_ge(turned, CHUNKS * t + c + 1)
                if j == 0 and not is_first(t):
                    act.wait_ge(pv_done, 2 * t + b - 1)
                act.copy(probs_t[b][:, :, P * j:P * j + P],
                         turn_bank[c % 2][:, :].rearrange("p (i n) -> p i n", i=JC)).then_inc(turned_kept, 1)

            def keep_sums(t, b):
                count = held(act, 2 * t + b + 1)
                act.wait_ge(params_loaded, DMA)
                act.wait_ge(pv_done, count)
                act.copy(half_of(MEAN, t, b), sums_bank(t, b)[0:C, :]).then_inc(sums_kept, 1)
                act.copy(half_of(VAR, t, b), sums_bank(t, b)[C:P, :]).then_inc(sums_kept, 1)

            def root(u):
                act.wait_ge(relu_done, u + 1)
                act.activation(tile_of(VAR, u), tile_of(VAR, u), ACT.Sqrt).then_inc(root_done, 1)

            act.wait_ge(params_loaded, DMA)
            act.copy(w_qk_hi[:, :, :], w_qk).then_inc(w_hi_ready, 1)
            act.activation(tanh_g[:, :], gates, ACT.Tanh).then_inc(gates_ready, 1)
            for part, whole, whole_done, part_done in ((x_hi, xn[:, :], xn_done, x_hi_done),
                                                       (c_hi, tile_of(CTX, 0), ctxn_done, c_hi_done)):
                act.wait_ge(whole_done, 1)
                act.copy(part[:, :], whole).then_inc(part_done, 1)
            keep_hi(0, 0)
            keep_hi(0, 1)
            act.wait_ge(k_hi_done, 1)
            act.copy(k_same[0][0:C, :], k_hi[0:C, :].bitcast(F32)).then_inc(stacked[0], DMA)
            act.copy(k_cross[0][C:P, :], k_hi[0:C, :].bitcast(F32)).then_inc(stacked[0], DMA)
            for c in range(AHEAD_E):
                exponentials(0, c)

            def body(t):
                for c in range(CHUNKS):
                    if c == 1 and has_next(t) and not is_first(t):
                        keep_hi(t + 1, 1)
                    if c + AHEAD_E < CHUNKS:
                        exponentials(t, c + AHEAD_E)
                    elif has_next(t):
                        exponentials(t + 1, c + AHEAD_E - CHUNKS)
                    if c == 0 and not is_first(t):
                        keep_sums(t - 1, 0)
                    if c < 2 and is_first(t):
                        keep_hi(t + 1, c)
                    if c > 0:
                        keep_turned(t, c - 1)
                    elif not is_first(t):
                        keep_turned(t - 1, CHUNKS - 1)
                    if c == 4 and not is_first(t):
                        keep_sums(t - 1, 1)
                    if c == 7 and has_second_next(t):
                        keep_hi(t + 2, 0)
                    if c == 6 and not has_next(t):
                        root(0)

            over_tiles(act, body)
            keep_turned(TILES - 1, CHUNKS - 1)
            root(1)

            def keep_y_hi(u, i):
                act.wait_ge(y_turned, u + 1)
                if not (isinstance(u, int) and u < 2):
                    act.wait_ge(ffn_done, u - 1)
                act.copy(yt_hi[i][:, :], score_bank[i][:, :]).then_inc(yt_hi_done, 1)

            def normalise_y(u):
                act.wait_ge(shift2_done, u + 1)
                if u >= 2:
                    act.wait_ge(y_turned, u - 1)
                act.activation(y[u % 2][:, :], tile_of(X, u), ACT.Identity, bias=shift2[:, u:u + 1],
                               scale=rstd2[:, u:u + 1]).then_inc(y_done, 1)

            root(2)
            root(3)
            keep_sums(TILES - 1, 0)
            root(4)
            normalise_y(0)
            normalise_y(1)
            keep_y_hi(0, 0)
            keep_y_hi(1, 1)
            normalise_y(2)
            keep_sums(TILES - 1, 1)
            root(5)
            normalise_y(3)
            root(6)
            for u in range(2, TILES):
                keep_y_hi(u, u % 2)
                if u == 3:
                    root(TILES - 1)
                if u + 2 < TILES:
                    normalise_y(u + 2)

        @block.vector
        def _(dve):
            def statistics(t):
                if isinstance(t, int) and t == 0:
                    dve.wait_ge(first_loaded[0][0], DMA)
                    dve.bn_stats(stats[:, 0, :], tile_of(X, 0)).then_inc(first_x_stats_done, 1)
                    dve.wait_ge(first_x_stats_done, 1)
                    dve.bn_aggr(mean_var[:, 0, :], stats[:, 0, :]).then_inc(first_x_mean_var_done, 1)
                    dve.wait_ge(first_x_mean_var_done, 1)
                    dve.tensor_scalar(var_eps[:, 0:1], mean_var[:, 0, 1:2], 1.0 + EPS, EPS * EPS,
                                      ALU.mult, ALU.add).then_inc(first_x_var_eps_done, 1)
                    dve.wait_ge(first_loaded[0][1], DMA)
                    dve.bn_stats(stats[:, 1, :], tile_of(CTX, 0)).then_inc(stats_done, 1)
                    dve.wait_ge(stats_done, 1)
                    dve.bn_aggr(mean_var[:, 1, :], stats[:, 1, :]).then_inc(mean_var_done, 1)
                    dve.wait_ge(mean_var_done, 1)
                    dve.tensor_scalar(var_eps[:, 1:2], mean_var[:, 1, 1:2], EPS, None,
                                      ALU.add).then_inc(var_eps_done, 1)
                    return
                if isinstance(t, int) and t < 3:
                    dve.wait_ge(first_loaded[t][0], DMA)
                    dve.bn_stats(stats[:, 0, :], tile_of(X, t))
                    dve.wait_ge(first_loaded[t][1], DMA)
                else:
                    count = held(dve, 2 * DMA * (t - 2))
                    dve.wait_ge(params_loaded, DMA)
                    dve.wait_ge(tile_loaded, count)
                    dve.bn_stats(stats[:, 0, :], tile_of(X, t))
                dve.bn_stats(stats[:, 1, :], tile_of(CTX, t)).then_inc(stats_done, 1)
                count = held(dve, t + 1)
                dve.wait_ge(params_loaded, DMA)
                dve.wait_ge(stats_done, count)
                dve.bn_aggr(mean_var[:, 0, :], stats[:, 0, :])
                dve.bn_aggr(mean_var[:, 1, :], stats[:, 1, :]).then_inc(mean_var_done, 1)
                dve.wait_ge(mean_var_done, t + 1)
                dve.tensor_scalar(var_eps[:, 0:1], mean_var[:, 0, 1:2], 1.0 + EPS, EPS * EPS, ALU.mult, ALU.add)
                dve.tensor_scalar(var_eps[:, 1:2], mean_var[:, 1, 1:2], EPS, None,
                                  ALU.add).then_inc(var_eps_done, 1)

            def normalise(t, which):
                if is_first(t) and which == 0:
                    dve.wait_ge(first_x_rstd_done, 1)
                else:
                    dve.wait_ge(rstd_done, t + 1)
                if which == 0:
                    if not is_first(t):
                        dve.wait_ge(x_lo_done, t)
                        dve.wait_ge(q_done, t)
                    dve.tensor_scalar(xn[:, :], tile_of(X, t), mean_var[:, 0, 0:1], rstd[:, 0:1],
                                      ALU.subtract, ALU.mult).then_inc(xn_done, 1)
                    if not is_first(t):
                        dve.wait_ge(xn_done, t + 1)
                        dve.tensor_copy(x_hi[:, :], xn[:, :]).then_inc(x_hi_done, 1)
                else:
                    if not is_first(t):
                        dve.wait_ge(k_done, t)
                    dve.tensor_scalar(tile_of(CTX, t), tile_of(CTX, t), mean_var[:, 1, 0:1], rstd[:, 1:2],
                                      ALU.subtract, ALU.mult).then_inc(ctxn_done, 1)
                    if not is_first(t):
                        count = held(dve, t + 1)
                        dve.wait_ge(params_loaded, DMA)
                        dve.wait_ge(ctxn_done, count)
                        dve.tensor_copy(c_hi[:, :], tile_of(CTX, t)).then_inc(c_hi_done, 1)

            def keep_lo(t, which):
                hi, lo, hi_done, lo_done = ((q_hi, q_lo, q_hi_done, q_lo_done),
                                            (k_hi, k_lo, k_hi_done, k_lo_done))[which]
                dve.wait_ge(hi_done, t + 1)
                dve.scalar_tensor_tensor(lo[:, :], bank_of(t, which)[:, :], b_qk[:, which:which + 1],
                                         hi[:, :].bitcast(F32), ALU.add, ALU.subtract).then_inc(lo_done, 1)

            def maximum(t, c):
                dve.wait_ge(scores_done, CHUNKS * t + c + 1)
                dve.tensor_reduce(neg_max[:, c:c + 1], score_bank[c % SBANKS][:, :], AX_X, ALU.max,
                                  negate=True).then_inc(max_done, 1)

            def reciprocal(t, c):
                dve.wait_ge(exp_done, CHUNKS * t + c + 1)
                dve.reciprocal(rden[:, c:c + 1], den[:, c:c + 1]).then_inc(rden_done, 1)

            def with_mean(t):
                dve.wait_ge(sums_kept, 4 * (t + 1))
                dve.scalar_tensor_tensor(tile_of(X, t), tile_of(MEAN, t), tanh_g[:, 0:1], tile_of(X, t),
                                         ALU.mult, ALU.add)

            def square_mean(t):
                if not is_first(t):
                    dve.wait_ge(var_done, t)
                dve.tensor_tensor(mean_sq[:, :], tile_of(MEAN, t), tile_of(MEAN, t),
                                  ALU.mult).then_inc(mean_squared, 1)

            def variance(t):
                dve.wait_ge(mean_squared, t + 1)
                dve.tensor_tensor(tile_of(VAR, t), tile_of(VAR, t), mean_sq[:, :],
                                  ALU.subtract).then_inc(var_done, 1)

            def relu(t):
                dve.wait_ge(var_done, t + 1)
                dve.tensor_scalar(tile_of(VAR, t), tile_of(VAR, t), 0.0, None, ALU.max).then_inc(relu_done, 1)

            def keep_values(t, b):
                dve.wait_ge(s_done, t + 1)
                if b == 1 and not is_first(t):
                    dve.wait_ge(pv_done, 2 * t)
                dve.tensor_tensor(values[:, :, b, 0, :],
                                  proj_bank[:, :].rearrange("p (i b c) -> p i b c", b=2, c=C)[:, :, b, :],
                                  b_s.unsqueeze(1).broadcast_to([P, JC, C]),
                                  ALU.add).then_inc(s_kept, 1)

            def after_attention(u):
                dve.wait_ge(scaled_done, u + 1)
                dve.scalar_tensor_tensor(tile_of(X, u), tile_of(CTX, u), tanh_g[:, 0:1], tile_of(X, u),
                                         ALU.mult, ALU.add).then_inc(x2_done, 1)

            def row_statistics(u):
                dve.wait_ge(x2_done, u + 1)
                dve.bn_stats(stats2[:, u, :], tile_of(X, u)).then_inc(stats2_done, 1)

            def finish_statistics(u):
                dve.wait_ge(stats2_done, u + 1)
                dve.bn_aggr(mean_var2[:, u, :], stats2[:, u, :]).then_inc(mean_var2_done, 1)
                dve.wait_ge(mean_var2_done, u + 1)
                dve.tensor_scalar(neg_mean2[:, u:u + 1], mean_var2[:, u, 0:1], -1.0, None, ALU.mult)
                dve.tensor_scalar(var_eps2[:, u:u + 1], mean_var2[:, u, 1:2], EPS, None,
                                  ALU.add).then_inc(var_eps2_done, 1)

            def scale_weights(g):
                if g >= 2:
                    dve.wait_ge(ffn_lo_done, g - 1)
                else:
                    dve.wait_ge(ffn_w_loaded, (1 + GROUPS) * DMA)
                dve.scalar_tensor_tensor(w_deq[g % 2][:, :], w_int[:, g, :], -QUANT_ZERO, sz[:, g, 0, :],
                                         ALU.add, ALU.mult).then_inc(w_scaled, 1)

            def weights_hi(g):
                dve.wait_ge(w_deq_done, g + 1)
                dve.tensor_copy(w_hi[:, g, :], w_deq[g % 2][:, :]).then_inc(ffn_hi_done, 1)

            statistics(0)
            normalise(0, 0)
            dve.wait_ge(w_hi_ready, 1)
            dve.tensor_tensor(w_qk_lo[:, :, :], w_qk, w_qk_hi[:, :, :].bitcast(F32),
                              ALU.subtract).then_inc(w_split, 1)
            normalise(0, 1)
            dve.wait_ge(x_hi_done, 1)
            dve.tensor_tensor(x_lo[:, :], xn[:, :], x_hi[:, :].bitcast(F32), ALU.subtract).then_inc(x_lo_done, 1)
            dve.wait_ge(c_hi_done, 1)
            dve.tensor_tensor(c_lo[:, :], tile_of(CTX, 0), c_hi[:, :].bitcast(F32),
                              ALU.subtract).then_inc(c_lo_done, 1)
            statistics(1)
            keep_lo(0, 0)
            keep_lo(0, 1)
            dve.wait_ge(k_lo_done, 1)
            dve.tensor_copy(k_same[0][C:P, :], k_lo[0:C, :].bitcast(F32)).then_inc(stacked[0], DMA)
            dve.tensor_copy(k_cross[0][0:C, :], k_lo[0:C, :].bitcast(F32)).then_inc(stacked[0], DMA)
            normalise(1, 0)
            dve.wait_ge(gates_ready, 1)
            for c in range(AHEAD_S):
                maximum(0, c)
                if c > 0:
                    reciprocal(0, c - 1)
            normalise(1, 1)

            def body(t):
                for c in range(CHUNKS):
                    if c + AHEAD_S < CHUNKS:
                        maximum(t, c + AHEAD_S)
                    elif has_next(t):
                        maximum(t + 1, c + AHEAD_S - CHUNKS)
                    if c + AHEAD_E < CHUNKS:
                        reciprocal(t, c + AHEAD_E)
                    elif has_next(t):
                        reciprocal(t + 1, c + AHEAD_E - CHUNKS)
                    if c == 0 and is_first(t):
                        keep_lo(1, 0)
                    if c == 1 and has_next(t):
                        keep_lo(t + 1, 1)
                    if not is_first(t):
                        if c == 5:
                            with_mean(t - 1)
                            square_mean(t - 1)
                        if c == 6:
                            variance(t - 1)
                        if c == 7:
                            relu(t - 1)
                    if c == 3:
                        keep_values(t, 0)
                    if c == 4:
                        keep_values(t, 1)
                    if has_second_next(t):
                        if c == 2:
                            statistics(t + 2)
                        if c == 4:
                            normalise(t + 2, 0)
                        if c == 6:
                            normalise(t + 2, 1)
                        if c == 7:
                            keep_lo(t + 2, 0)
                    else:
                        g = (t - TILES + 2) * (GROUPS // 2)
                        late = 3 * (t - TILES + 2)
                        if c == 0:
                            scale_weights(g)
                        if c == 1:
                            weights_hi(g)
                        if c == 5 - late:
                            scale_weights(g + 1)
                        if c == 6 - late:
                            weights_hi(g + 1)

            over_tiles(dve, body)
            dve.wait_ge(root_done, 1)
            dve.tensor_tensor(tile_of(CTX, 0), tile_of(CTX, 0), tile_of(VAR, 0), ALU.mult).then_inc(scaled_done, 1)
            after_attention(0)
            row_statistics(0)
            after_attention(1)
            finish_statistics(0)
            row_statistics(1)
            finish_statistics(1)
            after_attention(2)
            row_statistics(2)
            finish_statistics(2)

            def keep_y_lo(u, i):
                dve.wait_ge(yt_hi_done, u + 1)
                dve.tensor_tensor(yt_lo[i][:, :], score_bank[i][:, :], yt_hi[i][:, :].bitcast(F32),
                                  ALU.subtract).then_inc(yt_lo_done, 1)

            def add_ffn(u, i):
                dve.wait_ge(ffn_done, u + 1)
                if not (isinstance(u, int) and u < 2):
                    dve.wait_ge(stored[i], DMA // 2 * (u - i))
                dve.scalar_tensor_tensor(result[i][:, :], score_bank[2 + i][:, :], tanh_g[:, 1:2],
                                         tile_of(X, u), ALU.mult, ALU.add).then_inc(result_done, 1)

            keep_y_lo(0, 0)
            after_attention(3)
            row_statistics(3)
            keep_y_lo(1, 1)
            finish_statistics(3)
            for u in range(1, TILES):
                if u > 1:
                    keep_y_lo(u, u % 2)
                if u + 3 < TILES:
                    after_attention(u + 3)
                    row_statistics(u + 3)
                add_ffn(u - 1, (u - 1) % 2)
                if u + 3 < TILES:
                    finish_statistics(u + 3)
                if u == 1:
                    with_mean(TILES - 1)
                if u == 2:
                    relu(TILES - 1)
            add_ffn(TILES - 1, 1)

        @block.gpsimd
        def _(pool):
            def inverse_deviation(t):
                pool.wait_ge(var_eps_done, t + 1)
                pool.tensor_tensor(rstd[:, :], var_eps[:, :], power[:, :], ALU.pow).then_inc(rstd_done, 1)

            def split_lo(t, which):
                whole, hi, lo, hi_done, lo_done, used = (
                    (xn[:, :], x_hi, x_lo, x_hi_done, x_lo_done, q_done),
                    (tile_of(CTX, t), c_hi, c_lo, c_hi_done, c_lo_done, k_done))[which]
                pool.wait_ge(hi_done, t + 1)
                if not is_first(t):
                    pool.wait_ge(used, t)
                pool.tensor_tensor(lo[:, :], whole, hi[:, :].bitcast(F32), ALU.subtract).then_inc(lo_done, 1)

            def normalise_probs(t, c):
                count = held(pool, CHUNKS * t + c + 1)
                pool.wait_ge(ident_ready, 1)
                pool.wait_ge(rden_done, count)
                pool.tensor_scalar(probs[c % SBANKS][:, :], probs[c % SBANKS][:, :], rden[:, c:c + 1], 1.0,
                                   ALU.mult, ALU.mult).then_inc(probs_done, 1)

            def square_values(t, b):
                pool.wait_ge(s_kept, 2 * t + b + 1)
                pool.tensor_tensor(values[:, :, b, 1, :], values[:, :, b, 0, :], values[:, :, b, 0, :],
                                   ALU.mult).then_inc(s_squared, 1)

            def dequantise(g):
                pool.wait_ge(w_scaled, g + 1)
                pool.tensor_tensor(w_deq[g % 2][:, :], w_deq[g % 2][:, :], sz[:, g, 1, :],
                                   ALU.add).then_inc(w_deq_done, 1)

            def weights_lo(g):
                pool.wait_ge(ffn_hi_done, g + 1)
                pool.tensor_tensor(w_lo[:, g, :], w_deq[g % 2][:, :], w_hi[:, g, :].bitcast(F32),
                                   ALU.subtract).then_inc(ffn_lo_done, 1)

            pool.memset(ident[:, :], 0.0).then_inc(ident_zeroed, 1)
            pool.memset(power[:, :], -0.5).then_inc(consts_ready, 1)
            pool.wait_ge(ident_zeroed, 1)
            pool.affine_select(out=ident[:, :], in_=ident[:, :], compare_op=ALU.not_equal, fill=1.0, base=0,
                               pattern=[[-1, P]], channel_multiplier=1).then_inc(ident_ready, 1)
            pool.wait_ge(consts_ready, 1)
            pool.wait_ge(first_x_var_eps_done, 1)
            pool.tensor_tensor(rstd[:, 0:1], var_eps[:, 0:1], power[:, 0:1], ALU.pow).then_inc(first_x_rstd_done, 1)
            pool.wait_ge(var_eps_done, 1)
            pool.tensor_tensor(rstd[:, 1:2], var_eps[:, 1:2], power[:, 1:2], ALU.pow).then_inc(rstd_done, 1)
            inverse_deviation(1)
            split_lo(1, 0)
            for c in range(AHEAD_E):
                normalise_probs(0, c)
            split_lo(1, 1)

            def body(t):
                for c in range(CHUNKS):
                    if c + AHEAD_E < CHUNKS:
                        normalise_probs(t, c + AHEAD_E)
                    elif has_next(t):
                        normalise_probs(t + 1, c + AHEAD_E - CHUNKS)
                    if c == 3:
                        square_values(t, 0)
                    if c == 4:
                        square_values(t, 1)
                    if has_second_next(t):
                        if c == 2:
                            inverse_deviation(t + 2)
                        if c == 5:
                            split_lo(t + 2, 0)
                        if c == 6:
                            split_lo(t + 2, 1)
                    else:
                        g = (t - TILES + 2) * (GROUPS // 2)
                        late = 3 * (t - TILES + 2)
                        if c == 0:
                            dequantise(g)
                        if c == 1:
                            weights_lo(g)
                        if c == 5 - late:
                            dequantise(g + 1)
                        if c == 6 - late:
                            weights_lo(g + 1)

            over_tiles(pool, body)

            def scale_context(u):
                pool.wait_ge(root_done, u + 1)
                if u == 1:
                    pool.wait_ge(scaled_done, 1)
                pool.tensor_tensor(tile_of(CTX, u), tile_of(CTX, u), tile_of(VAR, u),
                                   ALU.mult).then_inc(scaled_done, 1)

            def inverse_deviation2(u):
                pool.wait_ge(var_eps2_done, u + 1)
                pool.tensor_tensor(rstd2[:, u:u + 1], var_eps2[:, u:u + 1], power[:, 0:1],
                                   ALU.pow).then_inc(rstd2_done, 1)
                pool.wait_ge(rstd2_done, u + 1)
                pool.tensor_tensor(shift2[:, u:u + 1], neg_mean2[:, u:u + 1], rstd2[:, u:u + 1],
                                   ALU.mult).then_inc(shift2_done, 1)

            def square_last_mean():
                pool.wait_ge(sums_kept, 4 * TILES)
                pool.wait_ge(var_done, TILES - 1)
                pool.tensor_tensor(mean_sq[:, :], tile_of(MEAN, TILES - 1), tile_of(MEAN, TILES - 1),
                                   ALU.mult).then_inc(mean_squared, 1)

            def last_variance():
                pool.wait_ge(mean_squared, TILES)
                pool.tensor_tensor(tile_of(VAR, TILES - 1), tile_of(VAR, TILES - 1), mean_sq[:, :],
                                   ALU.subtract).then_inc(var_done, 1)

            for u in (1, 2):
                scale_context(u)
            for u in (0, 1):
                inverse_deviation2(u)
            for u in range(2, TILES):
                if u + 1 < TILES:
                    scale_context(u + 1)
                inverse_deviation2(u)
                if u == 3:
                    square_last_mean()
                if u == 4:
                    last_variance()


def kernel(**inputs):
    import numpy as np
    import concourse.bacc as bacc
    from concourse.bass_utils import run_bass_kernel_spmd as run

    def laid(name, order=None):
        a = np.asarray(inputs[name])
        return np.ascontiguousarray(a if order is None else a.transpose(order))

    C = inputs["L0_xattn_Wq"].shape[0]
    params = np.zeros((P, 3 * P + 4 + C), np.float32)
    for half in range(2):
        rows = slice(C * half, C * half + C)
        for n, name in enumerate(("L0_xattn_Wq", "L0_xattn_Wk", "L0_xattn_Ws")):
            params[rows, P * n + C * half:P * n + C * half + C] = laid(name, (1, 0))
        for n, name in enumerate(("L0_xattn_bq", "L0_xattn_bk")):
            params[rows, 3 * P + n] = laid(name)
    for n, name in enumerate(("g_xattn", "g_ffn")):
        params[:, 3 * P + 2 + n] = laid(name)
    params[:, 3 * P + 4:] = laid("L0_xattn_bs_")
    arrays = {
        "x": laid("x"),
        "context": laid("ctx_4096"),
        "params": params,
        "weight_q_t": laid("L0_ffn_weight_q", (1, 0)),
        "scales_zeros": laid("L0_ffn_scales_and_zeros", (0, 2, 1)),
    }
    nc = bacc.Bacc("TRN2", target_bir_lowering=False, num_devices=1)
    args = [nc.dram_tensor(f"in_{n}", a.shape, mybir.dt.from_np(a.dtype), kind="ExternalInput").ap()
            for n, a in arrays.items()]
    out = nc.dram_tensor("out_0", arrays["x"].shape, F32, kind="ExternalOutput").ap()
    gated_attention_ffn(nc, *args, out)
    r = run(nc, [{f"in_{n}": a for n, a in arrays.items()}], core_ids=[0])
    return r.results[0]["out_0"]
```
